# Optimizing a Trainium2 kernel written in Bass

```python
import numpy as np
import jax
import jax.numpy as jnp

def _softmax(x, axis=-1):
    return jax.nn.softmax(x, axis=axis)

def _gelu(x):
    return jax.nn.gelu(x, approximate=True)

def _silu(x):
    return jax.nn.silu(x)

def _sigmoid(x):
    return jax.nn.sigmoid(x)

def _layernorm(x, axis=-1, eps=1e-05):
    m = jnp.mean(x, axis=axis, keepdims=True)
    v = jnp.var(x, axis=axis, keepdims=True)
    return (x - m) / jnp.sqrt(v + eps)

def _scatter_add(tgt, idx, src, axis=0):
    return tgt.at[idx].add(src)

def _segment_sum(src, seg, n):
    return jax.ops.segment_sum(src, seg, n)
kernel_name = 'mk_gnn_preln_d1_gnn_r8_8e445e'

def setup_inputs(seed: int=0):
    np.random.seed(seed)
    _w = jnp.asarray

    def _rec_inputs():
        import jax
        import jax.numpy as jnp
        _gk = jax.random.key(seed)
        x = -0.000202 + 1 * jax.random.normal(jax.random.fold_in(_gk, 1), (12500, 64), jnp.float32)
        src = jax.random.randint(jax.random.fold_in(_gk, 2), (400000,), 0, 12500, jnp.int32)
        dst = jnp.minimum((12500 * jax.random.uniform(jax.random.fold_in(_gk, 3), (400000,)) ** 2.0).astype(jnp.int32), 99999)
        _o = jnp.argsort(dst, stable=True)
        src = src[_o]
        dst = dst[_o]
        edge_weight1 = -0.000414295 + 0.999828 * jax.random.normal(jax.random.fold_in(_gk, 12), (400000, 1), jnp.float32)
        return (x, src, dst, edge_weight1)
    x, src, dst, edge_weight1 = _rec_inputs()

    def _L0_gnn_setup():
        import jax, jax.numpy as jnp
        import numpy as np
        N_NODES = 12500
        N_EDGES = 200000
        IN_FEATS = 64
        OUT_FEATS = 64
        EDGE_FEATS = 1
        key = jax.random.key(seed)
        ks = jax.random.split(key, 6)
        h = jax.random.normal(ks[0], (N_NODES, IN_FEATS), dtype=jnp.float32)
        e = jax.random.normal(ks[1], (N_EDGES, EDGE_FEATS), dtype=jnp.float32)
        src = jax.random.randint(ks[2], (N_EDGES,), 0, N_NODES, dtype=jnp.int32)
        dst = jax.random.randint(ks[3], (N_EDGES,), 0, N_NODES, dtype=jnp.int32)
        cat_dim = 2 * IN_FEATS + EDGE_FEATS
        W1 = jax.random.normal(ks[4], (cat_dim, OUT_FEATS), dtype=jnp.float32) / np.sqrt(cat_dim)
        b1 = jnp.zeros((OUT_FEATS,), dtype=jnp.float32)
        W2 = jax.random.normal(ks[5], (OUT_FEATS, OUT_FEATS), dtype=jnp.float32) / np.sqrt(OUT_FEATS)
        b2 = jnp.zeros((OUT_FEATS,), dtype=jnp.float32)
        return {'h': h, 'e': e, 'src': src, 'dst': dst, 'W1': W1, 'b1': b1, 'W2': W2, 'b2': b2}
    _L0_gnn_all = _L0_gnn_setup()
    _L0_gnn_in = {k: v for k, v in _L0_gnn_all.items() if k in ('W1', 'b1', 'W2', 'b2')}
    del _L0_gnn_all
    return {'x': x, 'src': src, 'dst': dst, 'edge_weight1': edge_weight1, 'L0_gnn_W1': _L0_gnn_in['W1'], 'L0_gnn_b1': _L0_gnn_in['b1'], 'L0_gnn_W2': _L0_gnn_in['W2'], 'L0_gnn_b2': _L0_gnn_in['b2']}

def reference(x, src, dst, edge_weight1, L0_gnn_W1, L0_gnn_b1, L0_gnn_W2, L0_gnn_b2):
    import jax
    import jax.numpy as jnp

    def _L0_gnn_ref(h, e, src, dst, W1, b1, W2, b2):
        import jax, jax.numpy as jnp
        import numpy as np
        N_NODES = 12500
        N_EDGES = 200000
        IN_FEATS = 64
        OUT_FEATS = 64
        EDGE_FEATS = 1
        x = jnp.concatenate([h[src], h[dst], e], axis=1)
        m = jax.nn.relu(x @ W1 + b1) @ W2 + b2
        h_new = jax.ops.segment_sum(m, dst, num_segments=h.shape[0])
        return h_new
    h = jnp.maximum(_layernorm(x, axis=-1), 0.0)
    x = x + _L0_gnn_ref(h, edge_weight1, src, dst, L0_gnn_W1, L0_gnn_b1, L0_gnn_W2, L0_gnn_b2)
    return x

_drawn_inputs = setup_inputs


def setup_inputs(seed=0):
    import zlib

    import numpy as np

    out = dict(_drawn_inputs(seed))
    spreads = {'L0_gnn_b1': (0.0, 0.1), 'L0_gnn_b2': (0.0, 0.1)}
    factors = {'edge_weight1': 4.986}
    for name, (base, spread) in spreads.items():
        noise = np.random.default_rng([zlib.crc32(name.encode()), seed]).standard_normal(out[name].shape)
        drawn = base * np.exp(spread * noise) if base else spread * noise
        out[name] = jnp.asarray(drawn.astype(out[name].dtype))
    for name, factor in factors.items():
        out[name] = (out[name] * factor).astype(out[name].dtype)
    return out
```

```python
import concourse.bass as bass
from concourse import mybir
from contextlib import ExitStack


def preln_gnn_layer(nc, x, src_cols, dst_cols, edge_cols, dst_flat, w1, b1, w2, b2, consts, out,
                    NODES, EDGES):
    fp32, bf16, i32 = mybir.dt.float32, mybir.dt.bfloat16, mybir.dt.int32
    ALU, ACT, AX = mybir.AluOpType, mybir.ActivationFunctionType, mybir.AxisListType
    ds = bass.ds

    P = 128
    F = 64
    TILES = EDGES // P
    WINDOWS = -(-NODES // P)
    TAIL = NODES - (WINDOWS - 1) * P
    EXTRA = WINDOWS - 1
    VISITS = TILES + EXTRA
    G = 6
    SLOTS = 3
    BATCHES = VISITS // G
    TURNS = BATCHES // SLOTS
    assert TILES * P == EDGES and BATCHES * G == VISITS and TURNS * SLOTS == BATCHES
    TILE_TURNS = TILES // (SLOTS * G)
    assert TILE_TURNS * SLOTS * G + G <= TILES and EXTRA < TILE_TURNS - 1
    COLS = VISITS + G
    GROUP = 8
    GROUPS = -(-WINDOWS // GROUP)
    EPS = 1e-5
    FAR = float(1 << 20)
    CHECK_P = 125
    CHECK_N = EDGES // CHECK_P
    assert CHECK_P * CHECK_N == EDGES and WINDOWS % 2 == 0
    SORT_SLOTS = 5
    SORT_TURNS = TILES // SORT_SLOTS
    assert SORT_SLOTS * SORT_TURNS == TILES

    def group_windows(g):
        return min(GROUP, WINDOWS - g * GROUP)

    a_table = nc.dram_tensor("a_table", (WINDOWS * P, F), fp32).ap()
    sorted_src = nc.dram_tensor("sorted_src", (EDGES, 1), i32).ap()
    sorted_dst = nc.dram_tensor("sorted_dst", (EDGES, 1), i32).ap()
    sorted_edge = nc.dram_tensor("sorted_edge", (EDGES, 1), fp32).ap()
    a_rows = a_table.rearrange("(w p) f -> p w f", p=P)

    with ExitStack() as ctx:
        def sb(name, shape, dt):
            return ctx.enter_context(nc.sbuf_tensor(name, shape, dt))

        def pb(name, shape, dt):
            return ctx.enter_context(nc.psum_tensor(name, shape, dt))

        def sem(name):
            return ctx.enter_context(nc.semaphore(name))

        cst = sb("cst", [P, 3 * P + 1], fp32)
        ident = cst[:, 0:P]
        iota = cst[:, P:2 * P]
        before = cst[:, 2 * P:3 * P]
        next_first = cst[:, 3 * P:3 * P + 1]
        ones = sb("ones", [P, P], fp32)
        ident_bf = sb("ident_bf", [P, P], bf16)
        eps_col = sb("eps_col", [P, 1], fp32)
        w1a = sb("w1a", [P, P], fp32)
        w1b = sb("w1b", [P, P], fp32)
        w2d = sb("w2d", [P, P], fp32)
        we_rows = sb("we_rows", [P, F], fp32)
        b1_rows = sb("b1_rows", [P, F], fp32)
        b2_rows = sb("b2_rows", [P, F], fp32)

        node_buf = sb("node_buf", [P, WINDOWS * (F + 1)], fp32)
        x_sb = node_buf[:, 0:WINDOWS * F].rearrange("p (w f) -> p w f", f=F)
        ends = sb("ends", [P, 2 * COLS], i32)
        dst_sb = ends[:, 0:COLS]
        src_sb = ends[:, COLS:2 * COLS]
        x_again = ends[:, 0:WINDOWS * F].bitcast(fp32).rearrange("p (w f) -> p w f", f=F)
        EARLY = COLS // (GROUP * F) * GROUP
        edge_sb = sb("edge_sb", [P, COLS], fp32)
        base_sb = sb("base_sb", [P, COLS], i32)
        rel_sb = base_sb[:, :].bitcast(fp32)
        win_row = sb("win_row", [1, G + COLS], i32)
        acc = [sb("acc", [P, WINDOWS, F + 1], fp32)[:, :, :], node_buf[:, :].rearrange("p (w f) -> p w f", f=F + 1)]
        b_table = sb("b_table", [P, WINDOWS, 3, F], bf16)

        stat = sb("stat", [P, 5, WINDOWS], fp32)
        viol = sb("viol", [P, 1], fp32)
        flag = sb("flag", [1, 1], i32)
        counts = sb("counts", [P, 1], fp32)
        diag = sb("diag", [P, EXTRA], fp32)
        extra_tile = sb("extra_tile", [1, EXTRA], i32)
        extra_base = sb("extra_base", [P, EXTRA], fp32)

        idx = sb("idx", [P, SLOTS, G], i32)
        a_edge = sb("a_edge", [P, SLOTS, G, F], fp32)
        loop_buf = sb("loop_buf", [P, 3, SLOTS * G * F], fp32)
        ew, pre, rest = (loop_buf[:, n, :].rearrange("p (s g f) -> p s g f", s=SLOTS, g=G) for n in range(3))
        a_stage = a_edge[:, :, :, :].rearrange("p s g f -> p (s g f)")[:, 0:2 * GROUP * F].rearrange("p (s n) -> p s n", s=2)
        square = loop_buf[:, 0, 0:2 * GROUP * F].rearrange("p (s n) -> p s n", s=2)
        b_rest = loop_buf[:, 1:3, :].rearrange("p a n -> p (a n)")[:, 0:3 * GROUP * F].rearrange("p (s n) -> p s n", s=3)
        onehot = sb("onehot", [P, SLOTS, G, P], bf16)
        onehot_t = sb("onehot_t", [P, SLOTS, G, P], bf16)
        r_hi = sb("r_hi", [P, SLOTS, G, F + 1], bf16)
        r_mid = sb("r_mid", [P, SLOTS, G, F], bf16)
        r_lo = sb("r_lo", [P, SLOTS, G, F], bf16)

        check_a = acc[0].rearrange("p w f -> p (w f)")[0:CHECK_P, 0:CHECK_N + 1].bitcast(i32)
        check_b = b_table[:, :, :, :].rearrange("p w s f -> p (w s f)").bitcast(fp32)[0:CHECK_P, 0:CHECK_N]
        h_t = x_sb[:, :, :].rearrange("p w f -> p (w f)").rearrange("p (k n) -> p k n", n=P)
        sums = b_table[:, :, :, :].rearrange("p w s f -> p (w s f)").bitcast(fp32)[:, 0:WINDOWS * F]
        less = b_table[:, :, :, :].rearrange("p w s f -> p (w s f)").bitcast(fp32)

        bank = [pb(f"bank{i}", [P, 512], fp32) for i in range(7)]
        bank_t = [bank[s][:, 0:G * P // 2].bitcast(bf16).rearrange("p (g n) -> p g n", g=G) for s in range(3)]
        bank_b = [bank[3 + s][:, 0:G * F].rearrange("p (g f) -> p g f", g=G) for s in range(3)]
        bank_seg = bank[6][:, 0:G * (F + 1)].rearrange("p (g f) -> p g f", g=G)

        s_cst = sem("s_cst")
        s_setup = sem("s_setup")
        s_x = [sem(f"s_x{i}") for i in range(2)]
        s_x_again = sem("s_x_again")
        s_flat = sem("s_flat")
        s_src = sem("s_src")
        s_dst = sem("s_dst")
        s_edge = sem("s_edge")
        s_base = sem("s_base")
        s_viol = sem("s_viol")
        s_violsum = sem("s_violsum")
        s_flag = sem("s_flag")
        s_ln = sem("s_ln")
        s_sq = sem("s_sq")
        s_std = sem("s_std")
        s_h = sem("s_h")
        s_ht_ps = sem("s_ht_ps")
        s_ht = sem("s_ht")
        s_a_ps = sem("s_a_ps")
        s_a_sb = sem("s_a_sb")
        s_a_out = [sem(f"s_a_out{i}") for i in range(2)]
        s_b_ps = sem("s_b_ps")
        s_bfull = sem("s_bfull")
        s_bhi = sem("s_bhi")
        s_brest = sem("s_brest")
        s_bmid = sem("s_bmid")
        s_blo = sem("s_blo")
        s_prep = sem("s_prep")
        s_count = sem("s_count")
        s_count_ps = sem("s_count_ps")
        s_extra = sem("s_extra")
        s_tables = sem("s_tables")
        s_extra_cols = [sem(f"s_extra_cols{i}") for i in range(3)]
        s_idx = [sem(f"s_idx{i}") for i in range(SLOTS)]
        s_gather = [sem(f"s_gather{i}") for i in range(SLOTS)]
        s_oh = sem("s_oh")
        s_t = sem("s_t")
        s_oht = sem("s_oht")
        s_bx = sem("s_bx")
        s_ew = sem("s_ew")
        s_u = sem("s_u")
        s_pre = sem("s_pre")
        s_hi = sem("s_hi")
        s_rest = sem("s_rest")
        s_mid = sem("s_mid")
        s_lo = sem("s_lo")
        s_seg = sem("s_seg")
        s_acc = sem("s_acc")
        s_sums = sem("s_sums")
        s_ft_ps = sem("s_ft_ps")
        s_ft = sem("s_ft")
        s_f_ps = sem("s_f_ps")
        s_fin = sem("s_fin")
        s_fx = sem("s_fx")
        s_out = sem("s_out")
        q_less = sem("q_less")
        q_off_ps = sem("q_off_ps")
        q_off = sem("q_off")
        q_oh = sem("q_oh")
        q_rank = sem("q_rank")
        q_pos = sem("q_pos")
        q_vec = sem("q_vec")
        q_cols = sem("q_cols")
        q_out = [sem(f"q_out{i}") for i in range(SORT_SLOTS)]
        q_in = sem("q_in")
        q_win = sem("q_win")

        s_off = square[:, 0, 0:WINDOWS]
        s_hot = square[:, 0, P:P + WINDOWS]
        s_place = square[:, 0, 2 * P:2 * P + WINDOWS]
        s_pick = square[:, 0, 3 * P:3 * P + WINDOWS]
        s_winf = square[:, 1, 0:1]
        s_posf = square[:, 1, 1:2]
        s_posi = square[:, 1, 2:4].bitcast(i32)
        s_posm = square[:, 1, 4:6].bitcast(i32)
        s_posx = square[:, 1, 8:8 + SORT_SLOTS].bitcast(i32)
        s_col_src = square[:, 1, 16:16 + SORT_SLOTS].bitcast(i32)
        s_col_dst = square[:, 1, 24:24 + SORT_SLOTS].bitcast(i32)
        s_col_edge = square[:, 1, 32:32 + SORT_SLOTS]

        def pool_sort(pool):
            placed = pool.alloc_register("placed")
            pool.reg_mov(placed, 1)
            with pool.Fori(0, SORT_TURNS) as turn:
                for slot in range(SORT_SLOTS):
                    pool.wait_ge(q_cols, placed)
                    pool.reg_alu(placed, placed, 1, ALU.add)
                    where = s_posx[:, slot:slot + 1]
                    for table, col in ((sorted_src, s_col_src), (sorted_dst, s_col_dst), (sorted_edge, s_col_edge)):
                        pool.indirect_dma_start(table, bass.IndirectOffsetOnAxis(where, 0), col[:, slot:slot + 1], None).then_inc(q_out[slot], 16)
            for slot in range(SORT_SLOTS):
                pool.wait_ge(q_out[slot], 16 * 3 * SORT_TURNS)
            cols = "(p t) o -> p (t o)"
            pool.dma_start(base_sb[:, 0:TILES], sorted_dst.rearrange(cols, p=P)[0:1, :].to_broadcast([P, TILES])).then_inc(q_in, 16)
            pool.dma_start(dst_sb[:, 0:TILES], sorted_dst.rearrange(cols, p=P)).then_inc(q_in, 16)
            pool.dma_start(src_sb[:, 0:TILES], sorted_src.rearrange(cols, p=P)).then_inc(q_in, 16)
            pool.dma_start(edge_sb[:, 0:TILES], sorted_edge.rearrange(cols, p=P)).then_inc(q_in, 16)

        def vector_sort(dve):
            nc.vector.memset(s_place, 0.0).then_inc(q_less, 1)
            dve.wait_ge(q_less, 1)
            with dve.Fori(1, WINDOWS) as w:
                dve.wait_ge(q_less, w * 2 - 1)
                nc.vector.tensor_scalar(s_winf, iota[:, ds(w, 1)], float(P), None, ALU.mult).then_inc(q_less, 1)
                dve.wait_ge(q_less, w * 2)
                nc.vector.tensor_scalar(less[:, 0:TILES], dst_sb[:, 0:TILES], s_winf, 0.0, ALU.is_lt, ALU.add,
                                        accum_out=s_place[:, ds(w, 1)]).then_inc(q_less, 1)
            dve.wait_ge(q_off_ps, 1)
            nc.vector.tensor_copy(s_off, bank[5][:, 0:WINDOWS]).then_inc(q_vec, 1)
            dve.wait_ge(q_vec, 1)
            nc.vector.tensor_scalar(less[:, 0:TILES].bitcast(i32), dst_sb[:, 0:TILES], 7, None, ALU.arith_shift_right).then_inc(q_vec, 1)
            STEPS = 7

            def place_turn(turn, first):
                for slot in range(SORT_SLOTS):
                    tile = turn * SORT_SLOTS + slot
                    done = tile * STEPS + 2
                    dve.wait_ge(q_vec, done)
                    nc.vector.tensor_copy(s_winf, less[:, ds(tile, 1)].bitcast(i32)).then_inc(q_vec, 1)
                    dve.wait_ge(q_vec, done + 1)
                    nc.vector.tensor_scalar(s_hot, iota[:, 0:WINDOWS], s_winf, None, ALU.is_equal).then_inc(q_oh, 1)
                    dve.wait_ge(q_rank, tile + 1)
                    nc.vector.tensor_tensor(s_pick, s_off, bank[5][:, 0:WINDOWS], ALU.add).then_inc(q_vec, 1)
                    dve.wait_ge(q_vec, done + 2)
                    nc.vector.tensor_tensor(s_pick, s_pick, s_hot, ALU.mult).then_inc(q_vec, 1)
                    nc.vector.tensor_tensor(s_off, s_off, bank[5][:, P:P + WINDOWS], ALU.add)
                    dve.wait_ge(q_vec, done + 3)
                    nc.vector.tensor_reduce(s_posf, s_pick, AX.X, ALU.add).then_inc(q_vec, 1)
                    dve.wait_ge(q_vec, done + 4)
                    nc.vector.tensor_copy(s_posi[:, 0:1], s_posf).then_inc(q_vec, 1)
                    dve.wait_ge(q_vec, done + 5)
                    nc.vector.tensor_scalar(s_posi[:, 1:2], s_posi[:, 0:1], 7, None, ALU.arith_shift_right)
                    nc.vector.tensor_scalar(s_posm[:, 0:1], s_posi[:, 0:1], P - 1, None, ALU.bitwise_and).then_inc(q_vec, 1)
                    dve.wait_ge(q_vec, done + 6)
                    if not first:
                        dve.wait_ge(q_out[slot], turn * (16 * 3))
                    nc.vector.scalar_tensor_tensor(s_posx[:, slot:slot + 1], s_posm[:, 0:1], float(TILES), s_posi[:, 1:2], ALU.mult, ALU.add).then_inc(q_vec, 1)
                    nc.vector.tensor_copy(s_col_src[:, slot:slot + 1], src_sb[:, ds(tile, 1)])
                    nc.vector.tensor_copy(s_col_dst[:, slot:slot + 1], dst_sb[:, ds(tile, 1)])
                    dve.wait_ge(q_vec, done + 7)
                    nc.vector.tensor_copy(s_col_edge[:, slot:slot + 1], edge_sb[:, ds(tile, 1)]).then_inc(q_cols, 1)

            place_turn(0, True)
            with dve.Fori(1, SORT_TURNS) as turn:
                place_turn(turn, False)
            dve.wait_ge(q_in, 16 * 4)

        def tensor_sort(pe):
            pe.wait_ge(q_less, 2 * WINDOWS - 1)
            nc.tensor.matmul(bank[5][:, 0:WINDOWS], ones[:, :], s_place, start=True, stop=True).then_inc(q_off_ps, 1)
            pe.wait_ge(q_vec, 1)
            with pe.Fori(0, TILES) as tile:
                pe.wait_ge(q_oh, tile + 1)
                nc.tensor.matmul(bank[5][:, 0:WINDOWS], before, s_hot, start=True, stop=True)
                nc.tensor.matmul(bank[5][:, P:P + WINDOWS], ones[:, :], s_hot, start=True, stop=True).then_inc(q_rank, 1)

        def load_windows(eng, regs, first):
            eng.reg_load(regs, win_row[0:1, ds(first, G)])
            return [eng.snap(r, min_val=0, max_val=WINDOWS - 1) for r in regs]

        def a_table_done(eng):
            for i in range(2):
                eng.wait_ge(s_a_out[i], 16 * len(range(i, GROUPS, 2)))

        block = ctx.enter_context(nc.Block())

        @block.sync
        def _(sp):
            sp.dma_start(cst[:, :], consts).then_inc(s_cst, 16)
            full = x[0:(WINDOWS - 1) * P, :].rearrange("(w p) f -> p w f", p=P)
            for g in range(GROUPS):
                n = group_windows(g)
                if g >= 2:
                    sp.wait_ge(s_x[g % 2], 16 * (g // 2))
                if g == GROUPS - 1:
                    sp.wait_ge(s_setup, 1)
                    if n > 1:
                        sp.dma_start(x_sb[:, g * GROUP:WINDOWS - 1, :], full[:, g * GROUP:WINDOWS - 1, :]).then_inc(s_x[g % 2], 16)
                    sp.dma_start(x_sb[0:TAIL, WINDOWS - 1, :], x[(WINDOWS - 1) * P:NODES, :]).then_inc(s_x[g % 2], 16)
                else:
                    sp.dma_start(x_sb[:, g * GROUP:g * GROUP + n, :], full[:, g * GROUP:g * GROUP + n, :]).then_inc(s_x[g % 2], 16)
            for g in range(GROUPS):
                n = group_windows(g)
                sp.wait_ge(s_a_sb, g + 1)
                sp.dma_start(a_rows[:, g * GROUP:g * GROUP + n, :],
                             a_stage[:, g % 2, 0:n * F].rearrange("p (w f) -> p w f", f=F)).then_inc(s_a_out[g % 2], 16)
            sp.wait_ge(s_tables, 1)
            def load_indices(turn, slot):
                sp.dma_start(idx[:, slot, :], src_sb[:, ds((turn * SLOTS + slot) * G, G)]).then_inc(s_idx[slot], 16)

            def load_turn(turn):
                for slot in range(SLOTS):
                    sp.wait_ge(s_gather[slot], turn * (16 * G))
                    load_indices(turn, slot)

            for slot in range(SLOTS):
                load_indices(0, slot)
            sp.wait_ge(s_extra, 1)
            sp.wait_ge(s_dst, 16)
            sp.wait_ge(s_edge, 16)
            with sp.Fori(1, EXTRA + 1) as turn:
                load_turn(turn)
                tile = sp.value_load(extra_tile[0:1, ds(turn - 1, 1)], min_val=0, max_val=TILES - 1)
                with nc.allow_non_contiguous_dma("one column of four-byte values"):
                    for n, cols in enumerate((src_sb, dst_sb, edge_sb)):
                        sp.dma_start(cols[:, ds(turn + (TILES - 1), 1)], cols[:, ds(tile, 1)]).then_inc(s_extra_cols[n], 16)
            for n in range(3):
                sp.wait_ge(s_extra_cols[n], 16 * EXTRA)
            with sp.Fori(EXTRA + 1, TURNS) as turn:
                load_turn(turn)
            sp.wait_ge(s_tables, 2)
            sp.dma_start(x_again[:, 0:EARLY, :], full[:, 0:EARLY, :]).then_inc(s_x_again, 16)
            for slot in range(SLOTS):
                sp.wait_ge(s_idx[slot], 16 * TURNS)
            sp.dma_start(x_again[:, EARLY:WINDOWS - 1, :], full[:, EARLY:WINDOWS - 1, :]).then_inc(s_x_again, 16)
            sp.dma_start(x_again[0:TAIL, WINDOWS - 1, :], x[(WINDOWS - 1) * P:NODES, :]).then_inc(s_x_again, 16)
            for g in range(GROUPS):
                n = group_windows(g)
                sp.wait_ge(s_fin, g + 1)
                last = g == GROUPS - 1
                m = n - 1 if last else n
                if m:
                    sp.dma_start(out[g * GROUP * P:(g * GROUP + m) * P, :].rearrange("(w p) f -> p w f", p=P),
                                 x_again[:, g * GROUP:g * GROUP + m, :]).then_inc(s_out, 16)
                if last:
                    sp.dma_start(out[(WINDOWS - 1) * P:NODES, :], x_again[0:TAIL, WINDOWS - 1, :]).then_inc(s_out, 16)
            sp.wait_ge(s_out, 16 * (GROUPS + 1))

        @block.scalar
        def _(act):
            act.wait_ge(s_setup, 1)
            for k in range(2):
                act.dma_start(w1a[k * F:(k + 1) * F, k * F:(k + 1) * F], w1[0:F, :]).then_inc(s_cst, 16)
                act.dma_start(w1b[k * F:(k + 1) * F, k * F:(k + 1) * F], w1[F:2 * F, :]).then_inc(s_cst, 16)
                act.dma_start(w2d[k * F:(k + 1) * F, k * F:(k + 1) * F], w2).then_inc(s_cst, 16)
            act.dma_start(we_rows[:, :], w1[2 * F:2 * F + 1, :].partition_broadcast(P) if False else w1[2 * F:2 * F + 1, :].to_broadcast([P, F])).then_inc(s_cst, 16)
            act.dma_start(b1_rows[:, :], b1.unsqueeze(0).to_broadcast([P, F])).then_inc(s_cst, 16)
            act.dma_start(b2_rows[:, :], b2.unsqueeze(0).to_broadcast([P, F])).then_inc(s_cst, 16)
            rows = dst_flat.rearrange("(p n) -> p n", p=CHECK_P)
            act.dma_start(check_a[:, 0:CHECK_N], rows).then_inc(s_flat, 16)
            with nc.allow_non_contiguous_dma("one value a row"):
                act.dma_start(check_a[0:CHECK_P - 1, CHECK_N:CHECK_N + 1], rows[1:CHECK_P, 0:1]).then_inc(s_flat, 16)
            act.dma_start(base_sb[:, 0:TILES], dst_cols[0:1, :].to_broadcast([P, TILES])).then_inc(s_base, 16)
            act.dma_start(dst_sb[:, 0:TILES], dst_cols).then_inc(s_dst, 16)
            act.dma_start(src_sb[:, 0:TILES], src_cols).then_inc(s_src, 16)
            act.dma_start(edge_sb[:, 0:TILES], edge_cols).then_inc(s_edge, 16)

            for g in range(GROUPS):
                n = group_windows(g)
                w = slice(g * GROUP, g * GROUP + n)
                act.wait_ge(s_ln, 3 * g + 2 if False else 5 * g + 3)
                if g >= 2:
                    act.wait_ge(s_ln, 5 * (g - 2) + 4)
                nc.scalar.activation(square[:, g % 2, 0:n * F], x_sb[:, w, :].rearrange("p w f -> p (w f)"), ACT.Square).then_inc(s_sq, 1)
                act.wait_ge(s_ln, 5 * g + 4)
                nc.scalar.activation(stat[:, 3, w], stat[:, 2, w], ACT.Sqrt, bias=eps_col[:, :], scale=1.0 / F).then_inc(s_std, 1)
            for g in range(GROUPS):
                n = group_windows(g)
                act.wait_ge(s_ht_ps, g + 1)
                nc.scalar.copy(h_t[:, g * 4:g * 4 + n // 2, :].rearrange("p k n -> p (k n)"), bank[g % 2][:, 0:n * F]).then_inc(s_ht, 1)
                act.wait_ge(s_a_ps, g + 1)
                if g >= 2:
                    act.wait_ge(s_a_out[g % 2], 16 * (g // 2))
                nc.scalar.copy(a_stage[:, g % 2, 0:n * F], bank[2 + g % 2][:, 0:n * F]).then_inc(s_a_sb, 1)
            for g in range(GROUPS):
                n = group_windows(g)
                w = slice(g * GROUP, g * GROUP + n)
                act.wait_ge(s_bfull, g + 1)
                nc.scalar.copy(b_table[:, w, 0, :], b_rest[:, 0, 0:n * F].rearrange("p (w f) -> p w f", f=F)).then_inc(s_bhi, 1)
                act.wait_ge(s_brest, g + 1)
                nc.scalar.copy(b_table[:, w, 1, :], b_rest[:, 1, 0:n * F].rearrange("p (w f) -> p w f", f=F)).then_inc(s_bmid, 1)

            def one_hot_out(batch, slot):
                act.wait_ge(s_t, batch + 1)
                nc.scalar.copy(onehot_t[:, slot, :, :], bank_t[slot]).then_inc(s_oht, 1)

            act.wait_ge(s_tables, 1)
            one_hot_out(0, 0)
            with act.Fori(0, TURNS) as turn:
                for slot in range(SLOTS):
                    batch = turn * SLOTS + slot
                    act.wait_ge(s_pre, batch + 1)
                    nc.scalar.activation(r_hi[:, slot, :, 0:F], pre[:, slot, :, :], ACT.Relu).then_inc(s_hi, 1)
                    act.wait_ge(s_rest, batch + 1)
                    nc.scalar.copy(r_mid[:, slot, :, :], rest[:, slot, :, :]).then_inc(s_mid, 1)
                    one_hot_out(batch + 1, (slot + 1) % SLOTS)
            for g in range(GROUPS):
                n = group_windows(g)
                act.wait_ge(s_ft_ps, g + 1)
                nc.scalar.copy(sums[:, g * GROUP * F:(g * GROUP + n) * F], bank[g % 2][:, 0:n * F]).then_inc(s_ft, 1)

        @block.gpsimd
        def _(pool):
            pool.wait_ge(s_flag, 1)
            unsorted = pool.value_load(flag[0:1, 0:1], min_val=0, max_val=1)
            with pool.If(unsorted):
                pool_sort(pool)
            a_table_done(pool)
            used = pool.alloc_register("used")
            pool.reg_mov(used, 1)

            def gather(turn, slot, first):
                pool.wait_ge(s_idx[slot], (turn + 1) * 16)
                if not first:
                    pool.wait_ge(s_u, used)
                    pool.reg_alu(used, used, 1, ALU.add)
                for v in range(G):
                    pool.indirect_dma_start(a_edge[:, slot, v, :], None, a_table,
                                            bass.IndirectOffsetOnAxis(idx[:, slot, v:v + 1], 0)).then_inc(s_gather[slot], 16)

            for slot in range(SLOTS):
                gather(0, slot, True)
            with pool.Fori(1, TURNS) as turn:
                for slot in range(SLOTS):
                    gather(turn, slot, False)
            pool.wait_ge(s_acc, G * (BATCHES + 1) + 2)
            for g in range(GROUPS):
                n = group_windows(g)
                w = slice(g * GROUP, g * GROUP + n)
                nc.gpsimd.tensor_tensor(sums[:, g * GROUP * F:(g * GROUP + n) * F].rearrange("p (w f) -> p w f", f=F), acc[0][:, w, 0:F], acc[1][:, w, 0:F], ALU.add).then_inc(s_sums, 1)

        @block.vector
        def _(dve):
            nc.vector.memset(w1a[:, :], 0.0)
            nc.vector.memset(w1b[:, :], 0.0)
            nc.vector.memset(w2d[:, :], 0.0)
            nc.vector.memset(x_sb[F:P, WINDOWS - 1, :], 0.0)
            nc.vector.memset(check_a[96:CHECK_P, CHECK_N:CHECK_N + 1], NODES)
            nc.vector.memset(eps_col[:, :], EPS)
            nc.vector.memset(ones[:, :], 1.0).then_inc(s_setup, 1)
            dve.wait_ge(s_cst, 16 * 10)
            nc.vector.tensor_copy(ident_bf[:, :], ident).then_inc(s_setup, 1)

            for g in range(GROUPS):
                n = group_windows(g)
                w = slice(g * GROUP, g * GROUP + n)
                many = [P, n, F]
                dve.wait_ge(s_x[g % 2], 16 * (g // 2 + 1) if g < GROUPS - 1 else 16 * (g // 2 + 1 + (n > 1)))
                nc.vector.tensor_reduce(stat[:, 0, w], x_sb[:, w, :], AX.X, ALU.add).then_inc(s_ln, 1)
                dve.wait_ge(s_ln, 5 * g + 1)
                nc.vector.tensor_scalar(stat[:, 1, w], stat[:, 0, w], 1.0 / F, None, ALU.mult).then_inc(s_ln, 1)
                dve.wait_ge(s_ln, 5 * g + 2)
                nc.vector.tensor_tensor(x_sb[:, w, :], x_sb[:, w, :], stat[:, 1, w].unsqueeze(2).to_broadcast(many), ALU.subtract).then_inc(s_ln, 1)
                dve.wait_ge(s_sq, g + 1)
                nc.vector.tensor_reduce(stat[:, 2, w], square[:, g % 2, 0:n * F].rearrange("p (w f) -> p w f", f=F), AX.X, ALU.add).then_inc(s_ln, 1)
                dve.wait_ge(s_std, g + 1)
                nc.vector.reciprocal(stat[:, 4, w], stat[:, 3, w]).then_inc(s_ln, 1)
                dve.wait_ge(s_ln, 5 * g + 5)
                nc.vector.scalar_tensor_tensor(x_sb[:, w, :], x_sb[:, w, :], 0.0, stat[:, 4, w].unsqueeze(2).to_broadcast(many),
                                               ALU.max, ALU.mult).then_inc(s_h, 1)

            dve.wait_ge(s_flat, 32)
            nc.vector.tensor_tensor(check_b, check_a[:, 0:CHECK_N], check_a[:, 1:CHECK_N + 1], ALU.is_gt).then_inc(s_viol, 1)
            nc.vector.memset(viol[:, :], 0.0).then_inc(s_viol, 1)
            dve.wait_ge(s_viol, 2)
            nc.vector.tensor_reduce(viol[0:CHECK_P, :], check_b, AX.X, ALU.max).then_inc(s_viol, 1)
            dve.wait_ge(s_violsum, 1)
            nc.vector.tensor_scalar(flag[0:1, 0:1], bank[4][0:1, 0:1], 1.0, None, ALU.min).then_inc(s_flag, 1)
            dve.wait_ge(s_base, 16)
            dve.wait_ge(s_dst, 16)
            dve.wait_ge(s_src, 16)
            dve.wait_ge(s_edge, 16)
            dve.wait_ge(s_flag, 1)
            unsorted = dve.value_load(flag[0:1, 0:1], min_val=0, max_val=1)
            with dve.If(unsorted):
                vector_sort(dve)
            nc.vector.memset(win_row[:, :], 0).then_inc(s_prep, 1)
            dve.wait_ge(s_prep, 1)
            nc.vector.tensor_scalar(win_row[0:1, G:G + TILES], base_sb[0:1, 0:TILES], 7, None, ALU.arith_shift_right).then_inc(s_prep, 1)
            nc.vector.tensor_copy(win_row[0:1, G + TILES:G + VISITS], iota[0:1, 1:WINDOWS]).then_inc(s_prep, 1)
            nc.vector.tensor_scalar(check_b[0:EXTRA, 0:TILES], base_sb[0:EXTRA, 0:TILES], next_first[0:EXTRA, :], 0.0,
                                    ALU.is_lt, ALU.add, accum_out=counts[0:EXTRA, :]).then_inc(s_prep, 1)
            dve.wait_ge(s_prep, 4)
            nc.vector.tensor_scalar(diag[0:EXTRA, :], ident[0:EXTRA, 0:EXTRA], counts[0:EXTRA, :], None, ALU.mult).then_inc(s_count, 1)
            nc.vector.tensor_scalar(base_sb[:, 0:TILES], base_sb[:, 0:TILES], -P, None, ALU.bitwise_and).then_inc(s_prep, 1)
            dve.wait_ge(s_prep, 5)
            nc.vector.tensor_tensor(rel_sb[:, 0:TILES], dst_sb[:, 0:TILES], base_sb[:, 0:TILES], ALU.subtract).then_inc(s_prep, 1)
            nc.vector.memset(rel_sb[:, VISITS:COLS], -1.0)
            nc.vector.memset(edge_sb[:, VISITS:COLS], 0.0)
            dve.wait_ge(s_count_ps, 1)
            tiles_before = bank[5][:, 0:EXTRA]
            nc.vector.tensor_scalar(extra_tile[0:1, :], bank[5][0:1, 0:EXTRA], -1.0, 0.0, ALU.add, ALU.max).then_inc(s_extra, 1)
            nc.vector.tensor_scalar(extra_base[:, :], tiles_before, 0.0, FAR, ALU.is_equal, ALU.mult).then_inc(s_prep, 1)
            dve.wait_ge(s_prep, 7)
            nc.vector.scalar_tensor_tensor(extra_base[:, :], iota[:, 1:WINDOWS], float(P), extra_base[:, :], ALU.mult, ALU.add).then_inc(s_prep, 1)

            for g in range(GROUPS):
                n = group_windows(g)
                w = slice(g * GROUP, g * GROUP + n)
                c = slice(0, n * F)
                dve.wait_ge(s_b_ps, g + 1)
                if g >= 1:
                    dve.wait_ge(s_bmid, g)
                nc.vector.tensor_tensor(b_rest[:, 0, c].rearrange("p (w f) -> p w f", f=F),
                                        bank[g % 2][:, c].rearrange("p (w f) -> p w f", f=F),
                                        b1_rows[:, :].unsqueeze(1).to_broadcast([P, n, F]), ALU.add).then_inc(s_bfull, 1)
                dve.wait_ge(s_bhi, g + 1)
                nc.vector.tensor_tensor(b_rest[:, 1, c].rearrange("p (w f) -> p w f", f=F),
                                        b_rest[:, 0, c].rearrange("p (w f) -> p w f", f=F), b_table[:, w, 0, :], ALU.subtract).then_inc(s_brest, 1)
                dve.wait_ge(s_bmid, g + 1)
                nc.vector.tensor_tensor(b_table[:, w, 2, :], b_rest[:, 1, c].rearrange("p (w f) -> p w f", f=F),
                                        b_table[:, w, 1, :], ALU.subtract).then_inc(s_blo, 1)
            nc.vector.memset(acc[0], 0.0).then_inc(s_acc, 1)
            nc.vector.memset(acc[1], 0.0).then_inc(s_acc, 1)
            nc.vector.memset(bank_seg, 0.0).then_inc(s_seg, 1)
            nc.vector.memset(r_hi[:, :, :, F:F + 1], 1.0).then_inc(s_tables, 1)

            window_regs = [dve.alloc_register(f"dve_window{v}") for v in range(G)]

            def one_hots(batch, slot):
                nc.vector.tensor_tensor(onehot[:, slot, :, :], rel_sb[:, ds(batch * G, G)].unsqueeze(2).to_broadcast([P, G, P]),
                                        iota.unsqueeze(1).to_broadcast([P, G, P]), ALU.is_equal).then_inc(s_oh, 1)

            def edge_terms(batch, slot):
                nc.vector.tensor_tensor(ew[:, slot, :, :], edge_sb[:, ds(batch * G, G)].unsqueeze(2).to_broadcast([P, G, F]),
                                        we_rows[:, :].unsqueeze(1).to_broadcast([P, G, F]), ALU.mult).then_inc(s_ew, 1)

            def accumulate(batch, windows, visits):
                for v in visits:
                    if v == 0:
                        dve.wait_ge(s_seg, batch + 1)
                    dve.wait_ge(s_acc, batch * G + (v + 1))
                    here = acc[v % 2][:, ds(windows[v], 1), :].rearrange("p w f -> p (w f)")
                    nc.vector.tensor_tensor(here, here, bank_seg[:, v, :], ALU.add).then_inc(s_acc, 1)

            one_hots(0, 0)
            edge_terms(0, 0)

            def turn_of_batches(turn):
                for slot in range(SLOTS):
                    batch = turn * SLOTS + slot
                    after = (slot + 1) % SLOTS
                    windows = load_windows(dve, window_regs, batch * G)
                    dve.wait_ge(s_ew, batch + 1)
                    dve.wait_ge(s_gather[slot], (turn + 1) * (16 * G))
                    nc.vector.tensor_tensor(pre[:, slot, :, :], ew[:, slot, :, :], a_edge[:, slot, :, :], ALU.add).then_inc(s_u, 1)
                    dve.wait_ge(s_u, batch + 1)
                    dve.wait_ge(s_bx, batch + 1)
                    nc.vector.tensor_tensor(pre[:, slot, :, :], pre[:, slot, :, :], bank_b[slot], ALU.add).then_inc(s_pre, 1)
                    one_hots(batch + 1, after)
                    accumulate(batch, windows, range(0, G // 2))
                    dve.wait_ge(s_hi, batch + 1)
                    nc.vector.scalar_tensor_tensor(rest[:, slot, :, :], pre[:, slot, :, :], 0.0, r_hi[:, slot, :, 0:F],
                                                   ALU.max, ALU.subtract).then_inc(s_rest, 1)
                    edge_terms(batch + 1, after)
                    accumulate(batch, windows, range(G // 2, G))
                    dve.wait_ge(s_mid, batch + 1)
                    nc.vector.tensor_tensor(r_lo[:, slot, :, :], rest[:, slot, :, :], r_mid[:, slot, :, :], ALU.subtract).then_inc(s_lo, 1)

            with dve.Fori(0, TILE_TURNS) as turn:
                turn_of_batches(turn)
            for n in range(3):
                dve.wait_ge(s_extra_cols[n], 16 * EXTRA)
            nc.vector.tensor_tensor(rel_sb[:, TILES:VISITS], dst_sb[:, TILES:VISITS], extra_base[:, :], ALU.subtract).then_inc(s_tables, 1)
            dve.wait_ge(s_tables, 2)
            with dve.Fori(TILE_TURNS, TURNS) as turn:
                turn_of_batches(turn)
            accumulate(BATCHES, load_windows(dve, window_regs, BATCHES * G), range(G))

            for g in range(GROUPS):
                n = group_windows(g)
                w = slice(g * GROUP, g * GROUP + n)
                many = [P, n, F]
                if g == 0:
                    dve.wait_ge(s_acc, G * (BATCHES + 1) + 2)
                    edges = acc[0][:, :, F:F + 1]
                    nc.vector.tensor_tensor(edges, edges, acc[1][:, :, F:F + 1], ALU.add).then_inc(s_fx, 1)
                    dve.wait_ge(s_fx, 1)
                edge_bias = b_rest[:, g % 2, 0:n * F].rearrange("p (w f) -> p w f", f=F)
                dve.wait_ge(s_acc, G * (BATCHES + 1) + 2)
                dve.wait_ge(s_x_again, 48)
                nc.vector.tensor_tensor(edge_bias, acc[0][:, w, F:F + 1].to_broadcast(many), b2_rows[:, :].unsqueeze(1).to_broadcast(many), ALU.mult).then_inc(s_fx, 1)
                dve.wait_ge(s_fx, 2 * g + 2)
                nc.vector.tensor_tensor(x_again[:, w, :], x_again[:, w, :], edge_bias, ALU.add).then_inc(s_fx, 1)
                dve.wait_ge(s_fx, 2 * g + 3)
                dve.wait_ge(s_f_ps, g + 1)
                nc.vector.tensor_tensor(x_again[:, w, :], x_again[:, w, :], bank[2 + g % 2][:, 0:n * F].rearrange("p (w f) -> p w f", f=F), ALU.add).then_inc(s_fin, 1)

        @block.tensor
        def _(pe):
            pe.wait_ge(s_setup, 2)
            for g in range(GROUPS):
                n = group_windows(g)
                pe.wait_ge(s_h, g + 1)
                if g >= 2:
                    pe.wait_ge(s_ht, g - 1)
                for k in range(n // 2):
                    w = g * GROUP + 2 * k
                    last = nc.tensor.transpose(bank[g % 2][:, k * P:(k + 1) * P], x_sb[:, w:w + 2, :].rearrange("p w f -> p (w f)"), ident)
                last.then_inc(s_ht_ps, 1)
                pe.wait_ge(s_ht, g + 1)
                if g >= 2:
                    pe.wait_ge(s_a_sb, g - 1)
                for k in range(n // 2):
                    last = nc.tensor.matmul(bank[2 + g % 2][:, k * P:(k + 1) * P], h_t[:, g * 4 + k, :], w1a[:, :], start=True, stop=True)
                last.then_inc(s_a_ps, 1)
            pe.wait_ge(s_viol, 3)
            nc.tensor.matmul(bank[4][:, 0:1], ones[:, :], viol[:, :], start=True, stop=True).then_inc(s_violsum, 1)
            pe.wait_ge(s_flag, 1)
            unsorted = pe.value_load(flag[0:1, 0:1], min_val=0, max_val=1)
            with pe.If(unsorted):
                tensor_sort(pe)
            pe.wait_ge(s_count, 1)
            nc.tensor.matmul(bank[5][:, 0:EXTRA], ones[0:EXTRA, :], diag[0:EXTRA, :], start=True, stop=True).then_inc(s_count_ps, 1)
            for g in range(GROUPS):
                n = group_windows(g)
                if g >= 2:
                    pe.wait_ge(s_bfull, g - 1)
                for k in range(n // 2):
                    last = nc.tensor.matmul(bank[g % 2][:, k * P:(k + 1) * P], h_t[:, g * 4 + k, :], w1b[:, :], start=True, stop=True)
                last.then_inc(s_b_ps, 1)
            pe.wait_ge(s_blo, GROUPS)

            def transposes(batch, slot):
                pe.wait_ge(s_oh, batch + 1)
                for v in range(G):
                    last = nc.tensor.transpose(bank_t[slot][:, v, :], onehot[:, slot, v, :], ident_bf[:, :])
                last.then_inc(s_t, 1)

            def expand(batch, slot, windows):
                pe.wait_ge(s_oht, batch + 1)
                for v in range(G):
                    for part in range(3):
                        last = nc.tensor.matmul(bank_b[slot][:, v, :], onehot_t[:, slot, v, :],
                                                b_table[:, ds(windows[v], 1), part, :].rearrange("p w f -> p (w f)"),
                                                start=part == 0, stop=part == 2)
                last.then_inc(s_bx, 1)

            window_regs = [pe.alloc_register(f"pe_window{v}") for v in range(G)]

            pe.wait_ge(s_tables, 1)
            transposes(0, 0)
            expand(0, 0, load_windows(pe, window_regs, G))
            with pe.Fori(0, TURNS) as turn:
                for slot in range(SLOTS):
                    batch = turn * SLOTS + slot
                    after = (slot + 1) % SLOTS
                    windows = load_windows(pe, window_regs, batch * G + 2 * G)
                    transposes(batch + 1, after)
                    expand(batch + 1, after, windows)
                    pe.wait_ge(s_lo, batch + 1)
                    pe.wait_ge(s_acc, batch * G + (G + 2))
                    for v in range(G):
                        nc.tensor.matmul(bank_seg[:, v, :], onehot[:, slot, v, :], r_hi[:, slot, v, :], start=True, stop=False)
                        nc.tensor.matmul(bank_seg[:, v, 0:F], onehot[:, slot, v, :], r_mid[:, slot, v, :], start=False, stop=False)
                        last = nc.tensor.matmul(bank_seg[:, v, 0:F], onehot[:, slot, v, :], r_lo[:, slot, v, :], start=False, stop=True)
                    last.then_inc(s_seg, 1)
            for g in range(GROUPS):
                n = group_windows(g)
                pe.wait_ge(s_sums, g + 1)
                if g >= 2:
                    pe.wait_ge(s_ft, g - 1)
                for k in range(n // 2):
                    w = g * GROUP + 2 * k
                    last = nc.tensor.transpose(bank[g % 2][:, k * P:(k + 1) * P], sums[:, w * F:(w + 2) * F], ident)
                last.then_inc(s_ft_ps, 1)
                pe.wait_ge(s_ft, g + 1)
                if g >= 2:
                    pe.wait_ge(s_fin, g - 1)
                for k in range(n // 2):
                    last = nc.tensor.matmul(bank[2 + g % 2][:, k * P:(k + 1) * P], sums[:, g * GROUP * F + k * P:g * GROUP * F + (k + 1) * P], w2d[:, :], start=True, stop=True)
                last.then_inc(s_f_ps, 1)

def kernel(x, src, dst, edge_weight1, L0_gnn_W1, L0_gnn_b1, L0_gnn_W2, L0_gnn_b2):
    import numpy as np
    import concourse.bacc as bacc
    from concourse import mybir as mb
    from concourse.bass_utils import run_bass_kernel_spmd

    P = 128
    nodes, feats = x.shape
    edges = src.shape[0]
    cols = lambda a: np.ascontiguousarray(np.asarray(a).reshape(-1, P).T)
    consts = np.concatenate([
        np.eye(P, dtype=np.float32),
        np.tile(np.arange(P, dtype=np.float32), (P, 1)),
        np.triu(np.ones((P, P), np.float32), 1),
        (P * np.arange(1, P + 1, dtype=np.float32))[:, None],
    ], axis=1)
    arrays = {
        "x_in": np.ascontiguousarray(x), "src_cols": cols(src), "dst_cols": cols(dst),
        "edge_cols": cols(edge_weight1), "dst_flat": np.ascontiguousarray(dst),
        "w1": np.ascontiguousarray(L0_gnn_W1), "b1": np.ascontiguousarray(L0_gnn_b1),
        "w2": np.ascontiguousarray(L0_gnn_W2), "b2": np.ascontiguousarray(L0_gnn_b2), "consts": consts,
    }
    nc = bacc.Bacc("TRN2", target_bir_lowering=False, num_devices=1)
    args = [nc.dram_tensor(n, a.shape, mb.dt.from_np(a.dtype), kind="ExternalInput").ap() for n, a in arrays.items()]
    out = nc.dram_tensor("out", (nodes, feats), mb.dt.float32, kind="ExternalOutput").ap()
    preln_gnn_layer(nc, *args, out, nodes, edges)
    r = run_bass_kernel_spmd(nc, [arrays], core_ids=[0])
    return r.results[0]["out"]
```

```python
import concourse.bass as bass
from concourse import mybir
from contextlib import ExitStack


def preln_gnn_layer(nc, x, src_cols, dst_cols, edge_cols, dst_flat, w1, b1, w2, b2, consts, out,
                    NODES, EDGES):
    fp32, bf16, i32 = mybir.dt.float32, mybir.dt.bfloat16, mybir.dt.int32
    ALU, ACT, AX = mybir.AluOpType, mybir.ActivationFunctionType, mybir.AxisListType
    ds = bass.ds

    P = 128
    F = 64
    TILES = EDGES // P
    WINDOWS = -(-NODES // P)
    TAIL = NODES - (WINDOWS - 1) * P
    EXTRA = WINDOWS - 1
    VISITS = TILES + EXTRA
    G = 6
    SLOTS = 3
    BATCHES = VISITS // G
    TURNS = BATCHES // SLOTS
    assert TILES * P == EDGES and BATCHES * G == VISITS and TURNS * SLOTS == BATCHES
    TILE_TURNS = TILES // (SLOTS * G)
    assert TILE_TURNS * SLOTS * G + G <= TILES and EXTRA < TILE_TURNS - 1
    COLS = VISITS + G
    GROUP = 8
    GROUPS = -(-WINDOWS // GROUP)
    EPS = 1e-5
    FAR = float(1 << 20)
    CHECK_P = 125
    CHECK_N = EDGES // CHECK_P
    assert CHECK_P * CHECK_N == EDGES and WINDOWS % 2 == 0
    CHECK_PIECES = 5
    PIECE = CHECK_N // CHECK_PIECES
    assert PIECE * CHECK_PIECES == CHECK_N
    SORT_SLOTS = 5
    SORT_TURNS = TILES // SORT_SLOTS
    assert SORT_SLOTS * SORT_TURNS == TILES

    def group_windows(g):
        return min(GROUP, WINDOWS - g * GROUP)

    a_table = nc.dram_tensor("a_table", (WINDOWS * P, F), fp32).ap()
    sorted_src = nc.dram_tensor("sorted_src", (EDGES, 1), i32).ap()
    sorted_dst = nc.dram_tensor("sorted_dst", (EDGES, 1), i32).ap()
    sorted_edge = nc.dram_tensor("sorted_edge", (EDGES, 1), fp32).ap()
    a_rows = a_table.rearrange("(w p) f -> p w f", p=P)

    with ExitStack() as ctx:
        def sb(name, shape, dt):
            return ctx.enter_context(nc.sbuf_tensor(name, shape, dt))

        def pb(name, shape, dt):
            return ctx.enter_context(nc.psum_tensor(name, shape, dt))

        def sem(name):
            return ctx.enter_context(nc.semaphore(name))

        cst = sb("cst", [P, 3 * P + 1], fp32)
        ident = cst[:, 0:P]
        iota = cst[:, P:2 * P]
        before = cst[:, 2 * P:3 * P]
        next_window = cst[:, 3 * P:3 * P + 1]
        ones = sb("ones", [P, P], fp32)
        ident_bf = sb("ident_bf", [P, P], bf16)
        eps_col = sb("eps_col", [P, 1], fp32)
        w1a = sb("w1a", [P, P], fp32)
        w1b = sb("w1b", [P, P], fp32)
        w2d = sb("w2d", [P, P], fp32)
        we_rows = sb("we_rows", [P, F], fp32)
        b1_rows = sb("b1_rows", [P, F], fp32)
        b2_rows = sb("b2_rows", [P, F], fp32)
        b1_part = sb("b1_part", [P, 3, F], fp32)
        b1_bf = sb("b1_bf", [P, 2, F], bf16)
        b1_split = sb("b1_split", [P, F], bf16)
        ones_bf = sb("ones_bf", [P, P], bf16)

        node_buf = sb("node_buf", [P, WINDOWS * (F + 1)], fp32)
        x_sb = node_buf[:, 0:WINDOWS * F].rearrange("p (w f) -> p w f", f=F)
        ends = sb("ends", [P, 2 * COLS], i32)
        dst_sb = ends[:, 0:COLS]
        src_sb = ends[:, COLS:2 * COLS]
        x_again = ends[:, 0:WINDOWS * F].bitcast(fp32).rearrange("p (w f) -> p w f", f=F)
        EARLY_PIECE = COLS // F // (TURNS - TILE_TURNS - 1)
        EARLY = EARLY_PIECE * (TURNS - TILE_TURNS - 1)
        LATE_PIECES = 6
        LATE_PIECE = -(-(WINDOWS - 1 - EARLY) // LATE_PIECES)
        edge_sb = sb("edge_sb", [P, COLS], fp32)
        base_sb = sb("base_sb", [P, COLS], i32)
        rel_sb = base_sb[:, :].bitcast(fp32)
        win_row = sb("win_row", [1, G + COLS], i32)
        acc = [sb("acc", [P, WINDOWS, F + 1], fp32)[:, :, :], node_buf[:, :].rearrange("p (w f) -> p w f", f=F + 1)]
        b_table = sb("b_table", [P, WINDOWS, 3, F], bf16)

        stat = sb("stat", [P, 5, WINDOWS], fp32)
        viol = sb("viol", [P, CHECK_PIECES + 2], fp32)
        zero_col = sb("zero_col", [P, 1], fp32)
        flag = sb("flag", [1, 1], i32)
        counts = sb("counts", [P, 1], fp32)
        diag = sb("diag", [P, EXTRA], fp32)
        extra_tile = sb("extra_tile", [1, EXTRA], i32)
        extra_base = sb("extra_base", [P, EXTRA], fp32)

        idx = sb("idx", [P, SLOTS, G], i32)
        a_edge = sb("a_edge", [P, SLOTS, G, F], fp32)
        loop_buf = sb("loop_buf", [P, 3, SLOTS * G * F], fp32)
        ew, pre, rest = (loop_buf[:, n, :].rearrange("p (s g f) -> p s g f", s=SLOTS, g=G) for n in range(3))
        square = loop_buf[:, 0, 0:2 * GROUP * F].rearrange("p (s n) -> p s n", s=2)
        b_rest = loop_buf[:, 1:3, :].rearrange("p a n -> p (a n)")[:, 0:4 * GROUP * F].rearrange("p (s n) -> p s n", s=4)
        a_stage = b_rest
        hot_buf = sb("hot_buf", [P, 2, SLOTS, G, P], bf16)
        onehot, onehot_t = hot_buf[:, 0, :, :, :], hot_buf[:, 1, :, :, :]
        is_before = hot_buf[:, :, :, :, :].rearrange("p a s g n -> p (a s g n)")[:, 0:TILES]
        r_hi = sb("r_hi", [P, SLOTS, G, F + 1], bf16)
        r_mid = sb("r_mid", [P, SLOTS, G, F], bf16)
        r_lo = sb("r_lo", [P, SLOTS, G, F], bf16)

        check_a = acc[0].rearrange("p w f -> p (w f)")[0:CHECK_P, 0:CHECK_N + 1].bitcast(i32)
        check_b = b_table[:, :, :, :].rearrange("p w s f -> p (w s f)").bitcast(fp32)[0:CHECK_P, 0:CHECK_N]
        check_d = check_b.bitcast(i32)
        h_t = x_sb[:, :, :].rearrange("p w f -> p (w f)").rearrange("p (k n) -> p k n", n=P)
        sums = b_table[:, :, :, :].rearrange("p w s f -> p (w s f)").bitcast(fp32)[:, 0:WINDOWS * F]
        less = b_table[:, :, :, :].rearrange("p w s f -> p (w s f)").bitcast(fp32)

        bank = [pb(f"bank{i}", [P, 512], fp32) for i in range(8)]
        EARLY_STEPS = [3, 6, 9]

        def bank_of_b(g):
            first = len(EARLY_STEPS)
            return bank[4 + g] if g < first else bank[(g - first) % 4]

        bank_t = [bank[s][:, 0:G * P // 2].bitcast(bf16).rearrange("p (g n) -> p g n", g=G) for s in range(3)]
        bank_b = [bank[3 + s][:, 0:G * F].rearrange("p (g f) -> p g f", g=G) for s in range(3)]
        bank_seg = bank[6][:, 0:G * (F + 1)].rearrange("p (g f) -> p g f", g=G)

        s_cst = sem("s_cst")
        s_w = sem("s_w")
        s_zero = sem("s_zero")
        s_setup = sem("s_setup")
        s_x = [sem(f"s_x{i}") for i in range(GROUPS)]
        s_x_early = sem("s_x_early")
        s_x_again = sem("s_x_again")
        s_flat = sem("s_flat")
        s_src = sem("s_src")
        s_dst = sem("s_dst")
        s_edge = sem("s_edge")
        s_base = sem("s_base")
        s_diff = sem("s_diff")
        s_least = sem("s_least")
        s_viol = sem("s_viol")
        s_ordered = sem("s_ordered")
        s_violsum = sem("s_violsum")
        s_flag = sem("s_flag")
        s_sum = sem("s_sum")
        s_mean = sem("s_mean")
        s_xc = sem("s_xc")
        s_sq = sem("s_sq")
        s_var = sem("s_var")
        s_inv = sem("s_inv")
        s_std = sem("s_std")
        s_h = sem("s_h")
        s_ht_ps = sem("s_ht_ps")
        s_ht = sem("s_ht")
        s_a_ps = sem("s_a_ps")
        s_a_sb = sem("s_a_sb")
        s_a_out = [sem(f"s_a_out{i}") for i in range(4)]
        s_b1 = sem("s_b1")
        s_b_ps = sem("s_b_ps")
        s_bhi = sem("s_bhi")
        s_brest = sem("s_brest")
        s_bmid = sem("s_bmid")
        s_blo = sem("s_blo")
        s_prep = sem("s_prep")
        s_window = sem("s_window")
        s_win_row = sem("s_win_row")
        s_count = sem("s_count")
        s_count_ps = sem("s_count_ps")
        s_extra = sem("s_extra")
        s_tables = sem("s_tables")
        s_extra_cols = [sem(f"s_extra_cols{i}") for i in range(3)]
        s_idx_first = sem("s_idx_first")
        s_idx = [sem(f"s_idx{i}") for i in range(SLOTS)]
        s_gather = [sem(f"s_gather{i}") for i in range(SLOTS)]
        s_oh = sem("s_oh")
        s_t = sem("s_t")
        s_oht = sem("s_oht")
        s_bx = sem("s_bx")
        s_ew = sem("s_ew")
        s_u = sem("s_u")
        s_pre = sem("s_pre")
        s_hi = sem("s_hi")
        s_rest = sem("s_rest")
        s_mid = sem("s_mid")
        s_lo = sem("s_lo")
        s_seg = sem("s_seg")
        s_acc = sem("s_acc")
        s_sums = sem("s_sums")
        s_ft_ps = sem("s_ft_ps")
        s_ft = sem("s_ft")
        s_f_ps = sem("s_f_ps")
        s_fin = sem("s_fin")
        s_edges = sem("s_edges")
        s_bias = sem("s_bias")
        s_pool_bias = sem("s_pool_bias")
        s_fx = sem("s_fx")
        s_out = sem("s_out")
        q_less = sem("q_less")
        q_off_ps = sem("q_off_ps")
        q_off = sem("q_off")
        q_oh = sem("q_oh")
        q_rank = sem("q_rank")
        q_pos = sem("q_pos")
        q_vec = sem("q_vec")
        q_cols = sem("q_cols")
        q_out = [sem(f"q_out{i}") for i in range(SORT_SLOTS)]
        q_in = sem("q_in")
        q_win = sem("q_win")

        s_off = square[:, 0, 0:WINDOWS]
        s_hot = square[:, 0, P:P + WINDOWS]
        s_place = square[:, 0, 2 * P:2 * P + WINDOWS]
        s_pick = square[:, 0, 3 * P:3 * P + WINDOWS]
        s_winf = square[:, 1, 0:1]
        s_posf = square[:, 1, 1:2]
        s_posi = square[:, 1, 2:4].bitcast(i32)
        s_posm = square[:, 1, 4:6].bitcast(i32)
        s_posx = square[:, 1, 8:8 + SORT_SLOTS].bitcast(i32)
        s_col_src = square[:, 1, 16:16 + SORT_SLOTS].bitcast(i32)
        s_col_dst = square[:, 1, 24:24 + SORT_SLOTS].bitcast(i32)
        s_col_edge = square[:, 1, 32:32 + SORT_SLOTS]

        def pool_sort(pool):
            placed = pool.alloc_register("placed")
            pool.reg_mov(placed, 1)
            with pool.Fori(0, SORT_TURNS) as turn:
                for slot in range(SORT_SLOTS):
                    pool.wait_ge(q_cols, placed)
                    pool.reg_alu(placed, placed, 1, ALU.add)
                    where = s_posx[:, slot:slot + 1]
                    for table, col in ((sorted_src, s_col_src), (sorted_dst, s_col_dst), (sorted_edge, s_col_edge)):
                        pool.indirect_dma_start(table, bass.IndirectOffsetOnAxis(where, 0), col[:, slot:slot + 1], None).then_inc(q_out[slot], 16)
            for slot in range(SORT_SLOTS):
                pool.wait_ge(q_out[slot], 16 * 3 * SORT_TURNS)
            cols = "(p t) o -> p (t o)"
            pool.dma_start(base_sb[:, 0:TILES], sorted_dst.rearrange(cols, p=P)[0:1, :].to_broadcast([P, TILES])).then_inc(q_in, 16)
            pool.dma_start(dst_sb[:, 0:TILES], sorted_dst.rearrange(cols, p=P)).then_inc(q_in, 16)
            pool.dma_start(src_sb[:, 0:TILES], sorted_src.rearrange(cols, p=P)).then_inc(q_in, 16)
            pool.dma_start(edge_sb[:, 0:TILES], sorted_edge.rearrange(cols, p=P)).then_inc(q_in, 16)

        def vector_sort(dve):
            dve.wait_ge(s_base, 16)
            dve.wait_ge(s_dst, 16)
            dve.wait_ge(s_src, 16)
            dve.wait_ge(s_edge, 16)
            nc.vector.memset(s_place, 0.0).then_inc(q_less, 1)
            dve.wait_ge(q_less, 1)
            with dve.Fori(1, WINDOWS) as w:
                dve.wait_ge(q_less, w * 2 - 1)
                nc.vector.tensor_scalar(s_winf, iota[:, ds(w, 1)], float(P), None, ALU.mult).then_inc(q_less, 1)
                dve.wait_ge(q_less, w * 2)
                nc.vector.tensor_scalar(less[:, 0:TILES], dst_sb[:, 0:TILES], s_winf, 0.0, ALU.is_lt, ALU.add,
                                        accum_out=s_place[:, ds(w, 1)]).then_inc(q_less, 1)
            dve.wait_ge(q_off_ps, 1)
            nc.vector.tensor_copy(s_off, bank[7][:, 0:WINDOWS]).then_inc(q_vec, 1)
            dve.wait_ge(q_vec, 1)
            nc.vector.tensor_scalar(less[:, 0:TILES].bitcast(i32), dst_sb[:, 0:TILES], 7, None, ALU.arith_shift_right).then_inc(q_vec, 1)
            STEPS = 7

            def place_turn(turn, first):
                for slot in range(SORT_SLOTS):
                    tile = turn * SORT_SLOTS + slot
                    done = tile * STEPS + 2
                    dve.wait_ge(q_vec, done)
                    nc.vector.tensor_copy(s_winf, less[:, ds(tile, 1)].bitcast(i32)).then_inc(q_vec, 1)
                    dve.wait_ge(q_vec, done + 1)
                    nc.vector.tensor_scalar(s_hot, iota[:, 0:WINDOWS], s_winf, None, ALU.is_equal).then_inc(q_oh, 1)
                    dve.wait_ge(q_rank, tile + 1)
                    nc.vector.tensor_tensor(s_pick, s_off, bank[7][:, 0:WINDOWS], ALU.add).then_inc(q_vec, 1)
                    dve.wait_ge(q_vec, done + 2)
                    nc.vector.tensor_tensor(s_pick, s_pick, s_hot, ALU.mult).then_inc(q_vec, 1)
                    nc.vector.tensor_tensor(s_off, s_off, bank[7][:, P:P + WINDOWS], ALU.add)
                    dve.wait_ge(q_vec, done + 3)
                    nc.vector.tensor_reduce(s_posf, s_pick, AX.X, ALU.add).then_inc(q_vec, 1)
                    dve.wait_ge(q_vec, done + 4)
                    nc.vector.tensor_copy(s_posi[:, 0:1], s_posf).then_inc(q_vec, 1)
                    dve.wait_ge(q_vec, done + 5)
                    nc.vector.tensor_scalar(s_posi[:, 1:2], s_posi[:, 0:1], 7, None, ALU.arith_shift_right)
                    nc.vector.tensor_scalar(s_posm[:, 0:1], s_posi[:, 0:1], P - 1, None, ALU.bitwise_and).then_inc(q_vec, 1)
                    dve.wait_ge(q_vec, done + 6)
                    if not first:
                        dve.wait_ge(q_out[slot], turn * (16 * 3))
                    nc.vector.scalar_tensor_tensor(s_posx[:, slot:slot + 1], s_posm[:, 0:1], float(TILES), s_posi[:, 1:2], ALU.mult, ALU.add).then_inc(q_vec, 1)
                    nc.vector.tensor_copy(s_col_src[:, slot:slot + 1], src_sb[:, ds(tile, 1)])
                    nc.vector.tensor_copy(s_col_dst[:, slot:slot + 1], dst_sb[:, ds(tile, 1)])
                    dve.wait_ge(q_vec, done + 7)
                    nc.vector.tensor_copy(s_col_edge[:, slot:slot + 1], edge_sb[:, ds(tile, 1)]).then_inc(q_cols, 1)

            place_turn(0, True)
            with dve.Fori(1, SORT_TURNS) as turn:
                place_turn(turn, False)
            dve.wait_ge(q_in, 16 * 4)

        def tensor_sort(pe):
            pe.wait_ge(q_less, 2 * WINDOWS - 1)
            nc.tensor.matmul(bank[7][:, 0:WINDOWS], ones[:, :], s_place, start=True, stop=True).then_inc(q_off_ps, 1)
            pe.wait_ge(q_vec, 1)
            with pe.Fori(0, TILES) as tile:
                pe.wait_ge(q_oh, tile + 1)
                nc.tensor.matmul(bank[7][:, 0:WINDOWS], before, s_hot, start=True, stop=True)
                nc.tensor.matmul(bank[7][:, P:P + WINDOWS], ones[:, :], s_hot, start=True, stop=True).then_inc(q_rank, 1)

        WINDOW_STEP, COUNT_STEP, REL_STEP, EXTRA_STEP, EDGE_STEP = 4, 6, 8, 9, 11

        def load_windows(eng, regs, first):
            eng.reg_load(regs, win_row[0:1, ds(first, G)])
            return [eng.snap(r, min_val=0, max_val=WINDOWS - 1) for r in regs]

        POOL_BIAS = GROUPS - 5

        def bias_of(g):
            return b_rest[:, g % 4, 0:group_windows(g) * F].rearrange("p (w f) -> p w f", f=F)

        def edge_bias(eng, g):
            n = group_windows(g)
            return eng.tensor_tensor(bias_of(g), acc[0][:, g * GROUP:g * GROUP + n, F:F + 1].to_broadcast([P, n, F]),
                                     b2_rows[:, :].unsqueeze(1).to_broadcast([P, n, F]), ALU.mult)

        def a_rows_out(eng, slot):
            eng.wait_ge(s_a_out[slot], 16 * len(range(slot, GROUPS, 4)))

        def a_table_done(eng):
            for slot in range(4):
                a_rows_out(eng, slot)

        block = ctx.enter_context(nc.Block())

        @block.sync
        def _(sp):
            sp.dma_start(cst[:, :], consts).then_inc(s_cst, 16)
            full = x[0:(WINDOWS - 1) * P, :].rearrange("(w p) f -> p w f", p=P)
            corners = [slice(k * F, (k + 1) * F) for k in range(2)]
            weights = [(w1a[c, c], w1[0:F, :]) for c in corners]
            weights += [(b1_rows[:, :], b1.unsqueeze(0).to_broadcast([P, F]))]
            weights += [(w1b[c, c], w1[F:2 * F, :]) for c in corners]
            weights += [(w2d[c, c], w2) for c in corners]
            weights += [(we_rows[:, :], w1[2 * F:2 * F + 1, :].to_broadcast([P, F])), (b2_rows[:, :], b2.unsqueeze(0).to_broadcast([P, F]))]
            for g in range(GROUPS):
                n = group_windows(g)
                if 1 <= g <= len(weights):
                    if g == 1:
                        sp.wait_ge(s_setup, 1)
                    sp.dma_start(*weights[g - 1]).then_inc(s_w, 16)
                if g == GROUPS - 1:
                    sp.wait_ge(s_setup, 1)
                    sp.dma_start(x_sb[:, g * GROUP:WINDOWS - 1, :], full[:, g * GROUP:WINDOWS - 1, :]).then_inc(s_x[g], 16)
                    sp.dma_start(x_sb[0:TAIL, WINDOWS - 1, :], x[(WINDOWS - 1) * P:NODES, :]).then_inc(s_x[g], 16)
                else:
                    sp.dma_start(x_sb[:, g * GROUP:g * GROUP + n, :], full[:, g * GROUP:g * GROUP + n, :]).then_inc(s_x[g], 16)
            rows = dst_flat.rearrange("(p n) -> p n", p=CHECK_P)
            sp.dma_start(check_a[:, 0:CHECK_N], rows).then_inc(s_flat, 16)
            with nc.allow_non_contiguous_dma("one value a row"):
                sp.dma_start(check_a[0:CHECK_P - 1, CHECK_N:CHECK_N + 1], rows[1:CHECK_P, 0:1]).then_inc(s_flat, 16)
            for g in range(GROUPS):
                n = group_windows(g)
                sp.wait_ge(s_a_sb, g + 1)
                sp.dma_start(a_rows[:, g * GROUP:g * GROUP + n, :],
                             a_stage[:, g % 4, 0:n * F].rearrange("p (w f) -> p w f", f=F)).then_inc(s_a_out[g % 4], 16)
                if g == 3:
                    sp.dma_start(src_sb[:, 0:TILES], src_cols).then_inc(s_src, 16)
            sp.dma_start(base_sb[:, 0:TILES], dst_cols[0:1, :].to_broadcast([P, TILES])).then_inc(s_base, 16)
            sp.dma_start(dst_sb[:, 0:TILES], dst_cols).then_inc(s_dst, 16)
            sp.dma_start(edge_sb[:, 0:TILES], edge_cols).then_inc(s_edge, 16)

            def load_turn(turn):
                for slot in range(SLOTS):
                    sp.wait_ge(s_gather[slot], turn * (16 * G))
                    sp.dma_start(idx[:, slot, :], src_sb[:, ds((turn * SLOTS + slot) * G, G)]).then_inc(s_idx[slot], 16)

            sp.wait_ge(s_extra, 1)
            sp.wait_ge(s_dst, 16)
            sp.wait_ge(s_edge, 16)
            with sp.Fori(1, EXTRA + 1) as turn:
                load_turn(turn)
                tile = sp.value_load(extra_tile[0:1, ds(turn - 1, 1)], min_val=0, max_val=TILES - 1)
                with nc.allow_non_contiguous_dma("one column of four-byte values"):
                    for n, cols in enumerate((src_sb, dst_sb, edge_sb)):
                        sp.dma_start(cols[:, ds(turn + (TILES - 1), 1)], cols[:, ds(tile, 1)]).then_inc(s_extra_cols[n], 16)
            for n in range(3):
                sp.wait_ge(s_extra_cols[n], 16 * EXTRA)
            with sp.Fori(EXTRA + 1, TILE_TURNS + 1) as turn:
                load_turn(turn)

            sp.wait_ge(s_tables, 2)
            with sp.Fori(TILE_TURNS + 1, TURNS) as turn:
                load_turn(turn)
                piece = ds((turn - (TILE_TURNS + 1)) * EARLY_PIECE, EARLY_PIECE)
                sp.dma_start(x_again[:, piece, :], full[:, piece, :]).then_inc(s_x_early, 16)
            for slot in range(SLOTS):
                sp.wait_ge(s_idx[slot], 16 * (TURNS - 1))
            for k in range(LATE_PIECES):
                w = slice(EARLY + k * LATE_PIECE, min(EARLY + (k + 1) * LATE_PIECE, WINDOWS - 1))
                if k >= 1:
                    sp.wait_ge(s_x_again, 16 * k)
                sp.dma_start(x_again[:, w, :], full[:, w, :]).then_inc(s_x_again, 16)
            sp.dma_start(x_again[0:TAIL, WINDOWS - 1, :], x[(WINDOWS - 1) * P:NODES, :]).then_inc(s_x_again, 16)
            for g in range(GROUPS):
                n = group_windows(g)
                sp.wait_ge(s_fin, g + 1)
                last = g == GROUPS - 1
                m = n - 1 if last else n
                if m:
                    sp.dma_start(out[g * GROUP * P:(g * GROUP + m) * P, :].rearrange("(w p) f -> p w f", p=P),
                                 x_again[:, g * GROUP:g * GROUP + m, :]).then_inc(s_out, 16)
                if last:
                    sp.dma_start(out[(WINDOWS - 1) * P:NODES, :], x_again[0:TAIL, WINDOWS - 1, :]).then_inc(s_out, 16)
            sp.wait_ge(s_out, 16 * (GROUPS + 1))

        @block.scalar
        def _(act):
            for step in range(GROUPS + 4):
                if step < GROUPS:
                    g, n = step, group_windows(step)
                    act.wait_ge(s_xc, g + 1)
                    if g >= 2:
                        act.wait_ge(s_var, g - 1)
                    nc.scalar.activation(square[:, g % 2, 0:n * F], x_sb[:, g * GROUP:g * GROUP + n, :].rearrange("p w f -> p (w f)"),
                                         ACT.Square).then_inc(s_sq, 1)
                if 1 <= step <= GROUPS:
                    g, n = step - 1, group_windows(step - 1)
                    w = slice(g * GROUP, g * GROUP + n)
                    act.wait_ge(s_var, g + 1)
                    nc.scalar.activation(stat[:, 3, w], stat[:, 2, w], ACT.Sqrt, bias=eps_col[:, :], scale=1.0 / F).then_inc(s_std, 1)
                if 3 <= step < GROUPS + 3:
                    g, n = step - 3, group_windows(step - 3)
                    act.wait_ge(s_ht_ps, g + 1)
                    nc.scalar.copy(h_t[:, g * 4:g * 4 + n // 2, :].rearrange("p k n -> p (k n)"), bank[g % 2][:, 0:n * F]).then_inc(s_ht, 1)
                if 4 <= step:
                    g, n = step - 4, group_windows(step - 4)
                    act.wait_ge(s_a_ps, g + 1)
                    if g >= 4:
                        act.wait_ge(s_a_out[g % 4], 16 * (g // 4))
                    nc.scalar.copy(a_stage[:, g % 4, 0:n * F], bank[2 + g % 2][:, 0:n * F]).then_inc(s_a_sb, 1)
            act.wait_ge(s_ordered, 1)
            for step in range(GROUPS + 1):
                if step < GROUPS:
                    g, n = step, group_windows(step)
                    act.wait_ge(s_b_ps, g + 1)
                    nc.scalar.copy(b_table[:, g * GROUP:g * GROUP + n, 0, :], bank_of_b(g)[:, 0:n * F].rearrange("p (w f) -> p w f", f=F)).then_inc(s_bhi, 1)
                    if g >= len(EARLY_STEPS):
                        cells = slice(g * GROUP * F, (g + 1) * GROUP * F if g < GROUPS - 1 else WINDOWS * (F + 1))
                        size = cells.stop - cells.start
                        last = nc.scalar.copy(node_buf[:, cells], zero_col[:, :].to_broadcast([P, size]))
                if step == REL_STEP:
                    act.wait_ge(s_brest, 3)
                    nc.scalar.copy(bank_seg, zero_col[:, :].unsqueeze(1).to_broadcast([P, G, F + 1])).then_inc(s_seg, 1)
                if step == COUNT_STEP:
                    act.wait_ge(s_window, 1)
                    act.dma_start(win_row[0:1, G:G + TILES], base_sb[0:1, 0:TILES]).then_inc(s_win_row, 16)
                if step >= 1:
                    g, n = step - 1, group_windows(step - 1)
                    act.wait_ge(s_brest, g + 1)
                    nc.scalar.copy(b_table[:, g * GROUP:g * GROUP + n, 1, :], b_rest[:, (g + 1) % 4, 0:n * F].rearrange("p (w f) -> p w f", f=F)).then_inc(s_bmid, 1)
            last.then_inc(s_acc, 1)

            def one_hot_out(batch, slot):
                act.wait_ge(s_t, batch + 1)
                nc.scalar.copy(onehot_t[:, slot, :, :], bank_t[slot]).then_inc(s_oht, 1)

            act.wait_ge(s_tables, 1)
            one_hot_out(0, 0)
            with act.Fori(0, TURNS) as turn:
                for slot in range(SLOTS):
                    batch = turn * SLOTS + slot
                    act.wait_ge(s_pre, batch + 1)
                    nc.scalar.activation(r_hi[:, slot, :, 0:F], pre[:, slot, :, :], ACT.Relu).then_inc(s_hi, 1)
                    one_hot_out(batch + 1, (slot + 1) % SLOTS)
                    act.wait_ge(s_rest, batch + 1)
                    nc.scalar.copy(r_mid[:, slot, :, :], rest[:, slot, :, :]).then_inc(s_mid, 1)
            for g in range(GROUPS):
                n = group_windows(g)
                act.wait_ge(s_ft_ps, g + 1)
                nc.scalar.copy(sums[:, g * GROUP * F:(g * GROUP + n) * F], bank[g % 2][:, 0:n * F]).then_inc(s_ft, 1)

        @block.gpsimd
        def _(pool):
            nc.gpsimd.memset(x_sb[F:P, WINDOWS - 1, :], 0.0).then_inc(s_zero, 1)
            pool.wait_ge(s_zero, 1)
            nc.gpsimd.memset(check_a[96:CHECK_P, CHECK_N:CHECK_N + 1], NODES).then_inc(s_zero, 1)
            pool.wait_ge(s_zero, 2)
            nc.gpsimd.memset(w1a[:, :], 0.0)
            nc.gpsimd.memset(w1b[:, :], 0.0)
            nc.gpsimd.memset(w2d[:, :], 0.0)
            nc.gpsimd.memset(eps_col[:, :], EPS)
            nc.gpsimd.memset(zero_col[:, :], 0.0)
            nc.gpsimd.memset(viol[:, :], 0.0)
            nc.gpsimd.memset(ones[:, :], 1.0).then_inc(s_setup, 1)
            pool.wait_ge(s_cst, 16)
            nc.gpsimd.memset(ones_bf[:, :], 1.0)
            nc.gpsimd.tensor_copy(ident_bf[:, :], ident).then_inc(s_setup, 1)
            for g in range(GROUPS):
                n = group_windows(g)
                w = slice(g * GROUP, g * GROUP + n)
                pool.wait_ge(s_mean, g + 1)
                nc.gpsimd.tensor_tensor(x_sb[:, w, :], x_sb[:, w, :], stat[:, 1, w].unsqueeze(2).to_broadcast([P, n, F]), ALU.subtract).then_inc(s_xc, 1)
                k = g - (GROUPS - CHECK_PIECES)
                if k >= 0:
                    c = slice(k * PIECE, (k + 1) * PIECE)
                    pool.wait_ge(s_flat, 32)
                    nc.gpsimd.tensor_tensor(check_d[:, c], check_a[:, k * PIECE + 1:(k + 1) * PIECE + 1], check_a[:, c], ALU.subtract).then_inc(s_diff, 1)
            pool.wait_ge(s_diff, CHECK_PIECES)
            nc.gpsimd.memset(acc[0], 0.0)
            pool.wait_ge(s_b_ps, len(EARLY_STEPS))
            nc.gpsimd.memset(node_buf[:, 0:len(EARLY_STEPS) * GROUP * F], 0.0).then_inc(s_acc, 1)
            pool.wait_ge(s_flag, 1)
            unsorted = pool.value_load(flag[0:1, 0:1], min_val=0, max_val=1)
            with pool.If(unsorted):
                pool_sort(pool)
            pool.wait_ge(s_src, 16)
            pool.wait_ge(s_ordered, 1)
            nc.gpsimd.tensor_copy(idx[:, :, :].rearrange("p s g -> p (s g)"), src_sb[:, 0:SLOTS * G]).then_inc(s_idx_first, 1)
            pool.wait_ge(s_idx_first, 1)
            a_table_done(pool)
            used = pool.alloc_register("used")
            pool.reg_mov(used, 1)

            def gather(turn, slot, first):
                if not first:
                    pool.wait_ge(s_idx[slot], turn * 16)
                    pool.wait_ge(s_u, used)
                    pool.reg_alu(used, used, 1, ALU.add)
                for v in range(G):
                    pool.indirect_dma_start(a_edge[:, slot, v, :], None, a_table,
                                            bass.IndirectOffsetOnAxis(idx[:, slot, v:v + 1], 0)).then_inc(s_gather[slot], 16)

            for slot in range(SLOTS):
                gather(0, slot, True)
            with pool.Fori(1, TURNS) as turn:
                for slot in range(SLOTS):
                    gather(turn, slot, False)
            pool.wait_ge(s_acc, G * (BATCHES + 1) + 2)
            for g in range(GROUPS):
                n = group_windows(g)
                w = slice(g * GROUP, g * GROUP + n)
                nc.gpsimd.tensor_tensor(sums[:, g * GROUP * F:(g * GROUP + n) * F].rearrange("p (w f) -> p w f", f=F), acc[0][:, w, 0:F], acc[1][:, w, 0:F], ALU.add).then_inc(s_sums, 1)
            pool.wait_ge(s_edges, 1)
            for g in range(POOL_BIAS, GROUPS):
                pool.wait_ge(s_fx, g - 3)
                edge_bias(nc.gpsimd, g).then_inc(s_pool_bias, 1)

        @block.vector
        def _(dve):
            for step in range(GROUPS + 2):
                if step < GROUPS:
                    g, n = step, group_windows(step)
                    w = slice(g * GROUP, g * GROUP + n)
                    dve.wait_ge(s_x[g], 16 if g < GROUPS - 1 else 32)
                    nc.vector.tensor_reduce(stat[:, 0, w], x_sb[:, w, :], AX.X, ALU.add).then_inc(s_sum, 1)
                    dve.wait_ge(s_sum, g + 1)
                    nc.vector.tensor_scalar(stat[:, 1, w], stat[:, 0, w], 1.0 / F, None, ALU.mult).then_inc(s_mean, 1)
                if 1 <= step <= GROUPS:
                    g, n = step - 1, group_windows(step - 1)
                    w = slice(g * GROUP, g * GROUP + n)
                    dve.wait_ge(s_sq, g + 1)
                    nc.vector.tensor_reduce(stat[:, 2, w], square[:, g % 2, 0:n * F].rearrange("p (w f) -> p w f", f=F), AX.X, ALU.add).then_inc(s_var, 1)
                if step >= 2:
                    g, n = step - 2, group_windows(step - 2)
                    w = slice(g * GROUP, g * GROUP + n)
                    dve.wait_ge(s_std, g + 1)
                    nc.vector.reciprocal(stat[:, 4, w], stat[:, 3, w]).then_inc(s_inv, 1)
                    dve.wait_ge(s_inv, g + 1)
                    nc.vector.scalar_tensor_tensor(x_sb[:, w, :], x_sb[:, w, :], 0.0, stat[:, 4, w].unsqueeze(2).to_broadcast([P, n, F]),
                                                   ALU.max, ALU.mult).then_inc(s_h, 1)
                if step == EARLY_STEPS[0]:
                    dve.wait_ge(s_w, 16 * 9)
                    dve.wait_ge(s_cst, 16)
                    nc.vector.tensor_copy(b1_bf[:, 0, :], b1_rows[:, :]).then_inc(s_b1, 1)
                    dve.wait_ge(s_b1, 1)
                    nc.vector.tensor_tensor(b1_part[:, 1, :], b1_rows[:, :], b1_bf[:, 0, :], ALU.subtract).then_inc(s_b1, 1)
                    nc.vector.tensor_scalar(b1_part[:, 0, :], b1_bf[:, 0, :], ident[:, 0:1], None, ALU.mult).then_inc(s_b1, 1)
                    dve.wait_ge(s_b1, 2)
                    nc.vector.tensor_copy(b1_bf[:, 1, :], b1_part[:, 1, :]).then_inc(s_b1, 1)
                    dve.wait_ge(s_b1, 4)
                    nc.vector.tensor_tensor(b1_part[:, 2, :], b1_part[:, 1, :], b1_bf[:, 1, :], ALU.subtract).then_inc(s_b1, 1)
                    nc.vector.scalar_tensor_tensor(b1_part[:, 0, :], b1_bf[:, 1, :], ident[:, 1:2], b1_part[:, 0, :], ALU.mult, ALU.add).then_inc(s_b1, 1)
                    dve.wait_ge(s_b1, 6)
                    nc.vector.scalar_tensor_tensor(b1_split[:, :], b1_part[:, 2, :], ident[:, 2:3], b1_part[:, 0, :], ALU.mult, ALU.add).then_inc(s_b1, 1)
                k = step - (GROUPS + 2 - CHECK_PIECES)
                if k >= 0:
                    dve.wait_ge(s_diff, k + 1)
                    nc.vector.tensor_reduce(viol[0:CHECK_P, 2 + k:3 + k], check_d[:, k * PIECE:(k + 1) * PIECE], AX.X, ALU.min).then_inc(s_least, 1)

            dve.wait_ge(s_least, CHECK_PIECES)
            dve.wait_ge(s_setup, 2)
            nc.vector.tensor_reduce(viol[0:CHECK_P, 1:2], viol[0:CHECK_P, 2:2 + CHECK_PIECES], AX.X, ALU.min).then_inc(s_viol, 1)
            dve.wait_ge(s_viol, 1)
            nc.vector.tensor_scalar(viol[0:CHECK_P, 0:1], viol[0:CHECK_P, 1:2], 0.0, None, ALU.is_lt).then_inc(s_viol, 1)
            dve.wait_ge(s_violsum, 1)
            nc.vector.tensor_scalar(flag[0:1, 0:1], bank[7][0:1, 0:1], 1.0, None, ALU.min).then_inc(s_flag, 1)
            nc.vector.memset(win_row[:, 0:G], 0)
            nc.vector.memset(win_row[:, G + VISITS:G + COLS], 0)
            nc.vector.tensor_copy(win_row[0:1, G + TILES:G + VISITS], iota[0:1, 1:WINDOWS])
            dve.wait_ge(s_flag, 1)
            unsorted = dve.value_load(flag[0:1, 0:1], min_val=0, max_val=1)
            with dve.If(unsorted):
                vector_sort(dve)
            nc.vector.memset(edge_sb[:, VISITS:COLS], 0.0).then_inc(s_ordered, 1)
            def one_hots(batch, slot):
                nc.vector.tensor_tensor(onehot[:, slot, :, :], rel_sb[:, ds(batch * G, G)].unsqueeze(2).to_broadcast([P, G, P]),
                                        iota.unsqueeze(1).to_broadcast([P, G, P]), ALU.is_equal).then_inc(s_oh, 1)

            def edge_terms(batch, slot):
                nc.vector.tensor_tensor(ew[:, slot, :, :], edge_sb[:, ds(batch * G, G)].unsqueeze(2).to_broadcast([P, G, F]),
                                        we_rows[:, :].unsqueeze(1).to_broadcast([P, G, F]), ALU.mult).then_inc(s_ew, 1)

            for step in range(GROUPS + 1):
                if step < GROUPS:
                    g, n = step, group_windows(step)
                    w = slice(g * GROUP, g * GROUP + n)
                    dve.wait_ge(s_bhi, g + 1)
                    if g >= 4:
                        dve.wait_ge(s_blo, g - 3)
                    else:
                        a_rows_out(dve, (g + 1) % 4)
                    nc.vector.tensor_tensor(b_rest[:, (g + 1) % 4, 0:n * F].rearrange("p (w f) -> p w f", f=F),
                                            bank_of_b(g)[:, 0:n * F].rearrange("p (w f) -> p w f", f=F), b_table[:, w, 0, :], ALU.subtract).then_inc(s_brest, 1)
                if step >= 1:
                    g, n = step - 1, group_windows(step - 1)
                    w = slice(g * GROUP, g * GROUP + n)
                    dve.wait_ge(s_bmid, g + 1)
                    nc.vector.tensor_tensor(b_table[:, w, 2, :], b_rest[:, (g + 1) % 4, 0:n * F].rearrange("p (w f) -> p w f", f=F),
                                            b_table[:, w, 1, :], ALU.subtract).then_inc(s_blo, 1)
                if step == WINDOW_STEP:
                    dve.wait_ge(s_base, 16)
                    nc.vector.tensor_scalar(base_sb[:, 0:TILES], base_sb[:, 0:TILES], 7, None, ALU.arith_shift_right).then_inc(s_window, 1)
                if step == COUNT_STEP:
                    dve.wait_ge(s_window, 1)
                    nc.vector.tensor_scalar(is_before[0:EXTRA, :], base_sb[0:EXTRA, 0:TILES], next_window[0:EXTRA, :], 0.0,
                                            ALU.is_lt, ALU.add, accum_out=counts[0:EXTRA, :]).then_inc(s_prep, 1)
                    dve.wait_ge(s_prep, 1)
                    nc.vector.tensor_scalar(diag[0:EXTRA, :], ident[0:EXTRA, 0:EXTRA], counts[0:EXTRA, :], None, ALU.mult).then_inc(s_count, 1)
                if step == REL_STEP:
                    dve.wait_ge(s_win_row, 16)
                    dve.wait_ge(s_dst, 16)
                    nc.vector.scalar_tensor_tensor(rel_sb[:, 0:TILES], base_sb[:, 0:TILES], -float(P), dst_sb[:, 0:TILES], ALU.mult, ALU.add).then_inc(s_prep, 1)
                    nc.vector.memset(rel_sb[:, VISITS:COLS], -1.0).then_inc(s_prep, 1)
                    dve.wait_ge(s_prep, 3)
                    one_hots(0, 0)
                if step == EXTRA_STEP:
                    dve.wait_ge(s_count_ps, 1)
                    nc.vector.tensor_scalar(extra_tile[0:1, :], bank[7][0:1, 0:EXTRA], -1.0, 0.0, ALU.add, ALU.max).then_inc(s_extra, 1)
                    nc.vector.tensor_scalar(extra_base[:, :], bank[7][:, 0:EXTRA], 0.0, FAR, ALU.is_equal, ALU.mult).then_inc(s_prep, 1)
                    dve.wait_ge(s_prep, 4)
                    nc.vector.scalar_tensor_tensor(extra_base[:, :], iota[:, 1:WINDOWS], float(P), extra_base[:, :], ALU.mult, ALU.add).then_inc(s_prep, 1)
                if step == EDGE_STEP:
                    dve.wait_ge(s_edge, 16)
                    edge_terms(0, 0)
                    nc.vector.memset(r_hi[:, :, :, F:F + 1], 1.0).then_inc(s_tables, 1)
            dve.wait_ge(s_acc, 2)
            dve.wait_ge(s_blo, GROUPS)

            window_regs = [dve.alloc_register(f"dve_window{v}") for v in range(G)]

            def accumulate(batch, windows, visits):
                for v in visits:
                    if v == 0:
                        dve.wait_ge(s_seg, batch + 1)
                    dve.wait_ge(s_acc, batch * G + (v + 1))
                    here = acc[v % 2][:, ds(windows[v], 1), :].rearrange("p w f -> p (w f)")
                    nc.vector.tensor_tensor(here, here, bank_seg[:, v, :], ALU.add).then_inc(s_acc, 1)

            def turn_of_batches(turn):
                for slot in range(SLOTS):
                    batch = turn * SLOTS + slot
                    after = (slot + 1) % SLOTS
                    windows = load_windows(dve, window_regs, batch * G)
                    one_hots(batch + 1, after)
                    edge_terms(batch + 1, after)
                    dve.wait_ge(s_ew, batch + 1)
                    dve.wait_ge(s_gather[slot], (turn + 1) * (16 * G))
                    nc.vector.tensor_tensor(pre[:, slot, :, :], ew[:, slot, :, :], a_edge[:, slot, :, :], ALU.add).then_inc(s_u, 1)
                    dve.wait_ge(s_u, batch + 1)
                    dve.wait_ge(s_bx, batch + 1)
                    nc.vector.tensor_tensor(pre[:, slot, :, :], pre[:, slot, :, :], bank_b[slot], ALU.add).then_inc(s_pre, 1)
                    accumulate(batch, windows, range(0, G // 2))
                    dve.wait_ge(s_hi, batch + 1)
                    nc.vector.scalar_tensor_tensor(rest[:, slot, :, :], pre[:, slot, :, :], 0.0, r_hi[:, slot, :, 0:F],
                                                   ALU.max, ALU.subtract).then_inc(s_rest, 1)
                    accumulate(batch, windows, range(G // 2, G))
                    dve.wait_ge(s_mid, batch + 1)
                    nc.vector.tensor_tensor(r_lo[:, slot, :, :], rest[:, slot, :, :], r_mid[:, slot, :, :], ALU.subtract).then_inc(s_lo, 1)

            with dve.Fori(0, TILE_TURNS) as turn:
                turn_of_batches(turn)
            for n in range(3):
                dve.wait_ge(s_extra_cols[n], 16 * EXTRA)
            nc.vector.tensor_tensor(rel_sb[:, TILES:VISITS], dst_sb[:, TILES:VISITS], extra_base[:, :], ALU.subtract).then_inc(s_tables, 1)
            dve.wait_ge(s_tables, 2)
            with dve.Fori(TILE_TURNS, TURNS) as turn:
                turn_of_batches(turn)
            accumulate(BATCHES, load_windows(dve, window_regs, BATCHES * G), range(G))

            dve.wait_ge(s_acc, G * (BATCHES + 1) + 2)
            edges = acc[0][:, :, F:F + 1]
            nc.vector.tensor_tensor(edges, edges, acc[1][:, :, F:F + 1], ALU.add).then_inc(s_edges, 1)
            dve.wait_ge(s_edges, 1)
            dve.wait_ge(s_x_early, 16 * (TURNS - TILE_TURNS - 1))
            dve.wait_ge(s_x_again, 16 * (LATE_PIECES + 1))
            for step in range(GROUPS + 2):
                if step < GROUPS:
                    g, n = step, group_windows(step)
                    w = slice(g * GROUP, g * GROUP + n)
                    if g < POOL_BIAS:
                        if g >= 4:
                            dve.wait_ge(s_fx, g - 3)
                        edge_bias(nc.vector, g).then_inc(s_bias, 1)
                        dve.wait_ge(s_bias, g + 1)
                    else:
                        dve.wait_ge(s_pool_bias, g - POOL_BIAS + 1)
                    nc.vector.tensor_tensor(x_again[:, w, :], x_again[:, w, :], bias_of(g), ALU.add).then_inc(s_fx, 1)
                if step >= 2:
                    g, n = step - 2, group_windows(step - 2)
                    w = slice(g * GROUP, g * GROUP + n)
                    dve.wait_ge(s_fx, g + 1)
                    dve.wait_ge(s_f_ps, g + 1)
                    nc.vector.tensor_tensor(x_again[:, w, :], x_again[:, w, :], bank[2 + g % 2][:, 0:n * F].rearrange("p (w f) -> p w f", f=F), ALU.add).then_inc(s_fin, 1)

        @block.tensor
        def _(pe):
            def b_group(g):
                n = group_windows(g)
                nc.tensor.matmul(bank_of_b(g)[:, 0:n * F], ones_bf[:, :], b1_split[:, :].unsqueeze(1).to_broadcast([P, n, F]), start=True, stop=False)
                for k in range(n // 2):
                    last = nc.tensor.matmul(bank_of_b(g)[:, k * P:(k + 1) * P], h_t[:, g * 4 + k, :], w1b[:, :], start=False, stop=k == n // 2 - 1)
                last.then_inc(s_b_ps, 1)

            pe.wait_ge(s_setup, 2)
            pe.wait_ge(s_w, 16 * 9)
            for step in range(GROUPS + 1):
                if step < GROUPS:
                    g, n = step, group_windows(step)
                    pe.wait_ge(s_h, g + 1)
                    if g >= 2:
                        pe.wait_ge(s_ht, g - 1)
                    for k in range(n // 2):
                        w = g * GROUP + 2 * k
                        last = nc.tensor.transpose(bank[g % 2][:, k * P:(k + 1) * P], x_sb[:, w:w + 2, :].rearrange("p w f -> p (w f)"), ident)
                    last.then_inc(s_ht_ps, 1)
                if step >= 1:
                    g, n = step - 1, group_windows(step - 1)
                    pe.wait_ge(s_ht, g + 1)
                    if g >= 2:
                        pe.wait_ge(s_a_sb, g - 1)
                    for k in range(n // 2):
                        last = nc.tensor.matmul(bank[2 + g % 2][:, k * P:(k + 1) * P], h_t[:, g * 4 + k, :], w1a[:, :], start=True, stop=True)
                    last.then_inc(s_a_ps, 1)
                if step in EARLY_STEPS:
                    if step == EARLY_STEPS[0]:
                        pe.wait_ge(s_b1, 7)
                    b_group(EARLY_STEPS.index(step))
            pe.wait_ge(s_viol, 2)
            nc.tensor.matmul(bank[7][:, 0:1], ones[:, :], viol[:, 0:1], start=True, stop=True).then_inc(s_violsum, 1)
            pe.wait_ge(s_flag, 1)
            unsorted = pe.value_load(flag[0:1, 0:1], min_val=0, max_val=1)
            with pe.If(unsorted):
                tensor_sort(pe)
            pe.wait_ge(s_ht, GROUPS)
            pe.wait_ge(s_a_sb, GROUPS)
            for g in range(len(EARLY_STEPS), GROUPS):
                if g >= len(EARLY_STEPS) + 4:
                    pe.wait_ge(s_brest, g - 3)
                b_group(g)
                if g == EXTRA_STEP:
                    pe.wait_ge(s_count, 1)
                    nc.tensor.matmul(bank[7][:, 0:EXTRA], ones[0:EXTRA, :], diag[0:EXTRA, :], start=True, stop=True).then_inc(s_count_ps, 1)
            def transposes(batch, slot):
                pe.wait_ge(s_oh, batch + 1)
                for v in range(G):
                    last = nc.tensor.transpose(bank_t[slot][:, v, :], onehot[:, slot, v, :], ident_bf[:, :])
                last.then_inc(s_t, 1)

            def expand(batch, slot, windows):
                pe.wait_ge(s_oht, batch + 1)
                for v in range(G):
                    for part in range(3):
                        last = nc.tensor.matmul(bank_b[slot][:, v, :], onehot_t[:, slot, v, :],
                                                b_table[:, ds(windows[v], 1), part, :].rearrange("p w f -> p (w f)"),
                                                start=part == 0, stop=part == 2)
                last.then_inc(s_bx, 1)

            window_regs = [pe.alloc_register(f"pe_window{v}") for v in range(G)]

            pe.wait_ge(s_brest, GROUPS)
            transposes(0, 0)
            pe.wait_ge(s_win_row, 16)
            windows = load_windows(pe, window_regs, G)
            pe.wait_ge(s_blo, GROUPS)
            expand(0, 0, windows)
            pe.wait_ge(s_tables, 1)
            with pe.Fori(0, TURNS) as turn:
                for slot in range(SLOTS):
                    batch = turn * SLOTS + slot
                    after = (slot + 1) % SLOTS
                    windows = load_windows(pe, window_regs, batch * G + 2 * G)
                    transposes(batch + 1, after)
                    expand(batch + 1, after, windows)
                    pe.wait_ge(s_lo, batch + 1)
                    pe.wait_ge(s_acc, batch * G + (G + 2))
                    for v in range(G):
                        nc.tensor.matmul(bank_seg[:, v, :], onehot[:, slot, v, :], r_hi[:, slot, v, :], start=True, stop=False)
                        nc.tensor.matmul(bank_seg[:, v, 0:F], onehot[:, slot, v, :], r_mid[:, slot, v, :], start=False, stop=False)
                        last = nc.tensor.matmul(bank_seg[:, v, 0:F], onehot[:, slot, v, :], r_lo[:, slot, v, :], start=False, stop=True)
                    last.then_inc(s_seg, 1)
            for step in range(GROUPS + 1):
                if step < GROUPS:
                    g, n = step, group_windows(step)
                    pe.wait_ge(s_sums, g + 1)
                    if g >= 2:
                        pe.wait_ge(s_ft, g - 1)
                    for k in range(n // 2):
                        w = g * GROUP + 2 * k
                        last = nc.tensor.transpose(bank[g % 2][:, k * P:(k + 1) * P], sums[:, w * F:(w + 2) * F], ident)
                    last.then_inc(s_ft_ps, 1)
                if step >= 1:
                    g, n = step - 1, group_windows(step - 1)
                    pe.wait_ge(s_ft, g + 1)
                    if g >= 2:
                        pe.wait_ge(s_fin, g - 1)
                    for k in range(n // 2):
                        last = nc.tensor.matmul(bank[2 + g % 2][:, k * P:(k + 1) * P], sums[:, g * GROUP * F + k * P:g * GROUP * F + (k + 1) * P], w2d[:, :], start=True, stop=True)
                    last.then_inc(s_f_ps, 1)

def kernel(x, src, dst, edge_weight1, L0_gnn_W1, L0_gnn_b1, L0_gnn_W2, L0_gnn_b2):
    import numpy as np
    import concourse.bacc as bacc
    from concourse import mybir as mb
    from concourse.bass_utils import run_bass_kernel_spmd

    P = 128
    nodes, feats = x.shape
    edges = src.shape[0]
    cols = lambda a: np.ascontiguousarray(np.asarray(a).reshape(-1, P).T)
    consts = np.concatenate([
        np.eye(P, dtype=np.float32),
        np.tile(np.arange(P, dtype=np.float32), (P, 1)),
        np.triu(np.ones((P, P), np.float32), 1),
        np.arange(1, P + 1, dtype=np.float32)[:, None],
    ], axis=1)
    arrays = {
        "x_in": np.ascontiguousarray(x), "src_cols": cols(src), "dst_cols": cols(dst),
        "edge_cols": cols(edge_weight1), "dst_flat": np.ascontiguousarray(dst),
        "w1": np.ascontiguousarray(L0_gnn_W1), "b1": np.ascontiguousarray(L0_gnn_b1),
        "w2": np.ascontiguousarray(L0_gnn_W2), "b2": np.ascontiguousarray(L0_gnn_b2), "consts": consts,
    }
    nc = bacc.Bacc("TRN2", target_bir_lowering=False, num_devices=1)
    args = [nc.dram_tensor(n, a.shape, mb.dt.from_np(a.dtype), kind="ExternalInput").ap() for n, a in arrays.items()]
    out = nc.dram_tensor("out", (nodes, feats), mb.dt.float32, kind="ExternalOutput").ap()
    preln_gnn_layer(nc, *args, out, nodes, edges)
    r = run_bass_kernel_spmd(nc, [arrays], core_ids=[0])
    return r.results[0]["out"]
```

```python
import concourse.bass as bass
from concourse import mybir
from contextlib import ExitStack


def preln_gnn_layer(nc, x, src_cols, dst_cols, edge_cols, dst_flat, w1, b1, w2, b2, consts, out,
                    NODES, EDGES):
    fp32, bf16, i32 = mybir.dt.float32, mybir.dt.bfloat16, mybir.dt.int32
    ALU, ACT, AX = mybir.AluOpType, mybir.ActivationFunctionType, mybir.AxisListType
    ds = bass.ds

    P = 128
    F = 64
    TILES = EDGES // P
    WINDOWS = -(-NODES // P)
    TAIL = NODES - (WINDOWS - 1) * P
    EXTRA = WINDOWS - 1
    VISITS = TILES + EXTRA
    G = 6
    SLOTS = 3
    BATCHES = VISITS // G
    TURNS = BATCHES // SLOTS
    assert TILES * P == EDGES and BATCHES * G == VISITS and TURNS * SLOTS == BATCHES
    TILE_TURNS = TILES // (SLOTS * G)
    assert TILE_TURNS * SLOTS * G + G <= TILES and EXTRA < TILE_TURNS - 1
    COLS = VISITS + G
    GROUP = 8
    GROUPS = -(-WINDOWS // GROUP)
    EPS = 1e-5
    FAR = float(1 << 20)
    CHECK_P = 125
    CHECK_N = EDGES // CHECK_P
    assert CHECK_P * CHECK_N == EDGES and WINDOWS % 2 == 0
    CHECK_PIECES = 5
    PIECE = CHECK_N // CHECK_PIECES
    assert PIECE * CHECK_PIECES == CHECK_N
    SORT_SLOTS = 5
    SORT_TURNS = TILES // SORT_SLOTS
    assert SORT_SLOTS * SORT_TURNS == TILES

    def group_windows(g):
        return min(GROUP, WINDOWS - g * GROUP)

    a_table = nc.dram_tensor("a_table", (WINDOWS * P, F), fp32).ap()
    sorted_src = nc.dram_tensor("sorted_src", (EDGES, 1), i32).ap()
    sorted_dst = nc.dram_tensor("sorted_dst", (EDGES, 1), i32).ap()
    sorted_edge = nc.dram_tensor("sorted_edge", (EDGES, 1), fp32).ap()
    a_rows = a_table.rearrange("(w p) f -> p w f", p=P)

    with ExitStack() as ctx:
        def sb(name, shape, dt):
            return ctx.enter_context(nc.sbuf_tensor(name, shape, dt))

        def pb(name, shape, dt):
            return ctx.enter_context(nc.psum_tensor(name, shape, dt))

        def sem(name):
            return ctx.enter_context(nc.semaphore(name))

        cst = sb("cst", [P, 3 * P + 1], fp32)
        ident = cst[:, 0:P]
        iota = cst[:, P:2 * P]
        before = cst[:, 2 * P:3 * P]
        next_window = cst[:, 3 * P:3 * P + 1]
        ones = sb("ones", [P, P], fp32)
        ident_bf = sb("ident_bf", [P, P], bf16)
        eps_col = sb("eps_col", [P, 1], fp32)
        w1a = sb("w1a", [P, P], fp32)
        w1b = sb("w1b", [P, P], fp32)
        w2d = sb("w2d", [P, P], fp32)
        we_rows = sb("we_rows", [P, F], fp32)
        b1_rows = sb("b1_rows", [P, F], fp32)
        b2_rows = sb("b2_rows", [P, F], fp32)
        b1_part = sb("b1_part", [P, 3, F], fp32)
        b1_bf = sb("b1_bf", [P, 2, F], bf16)
        b1_split = sb("b1_split", [P, F], bf16)
        ones_bf = sb("ones_bf", [P, P], bf16)

        node_buf = sb("node_buf", [P, WINDOWS * (F + 1)], fp32)
        x_sb = node_buf[:, 0:WINDOWS * F].rearrange("p (w f) -> p w f", f=F)
        ends = sb("ends", [P, 2 * COLS], i32)
        dst_sb = ends[:, 0:COLS]
        src_sb = ends[:, COLS:2 * COLS]
        x_again = ends[:, 0:WINDOWS * F].bitcast(fp32).rearrange("p (w f) -> p w f", f=F)
        EARLY_PIECE = COLS // F // (TURNS - TILE_TURNS - 1)
        EARLY = EARLY_PIECE * (TURNS - TILE_TURNS - 1)
        LATE_PIECES = 6
        LATE_PIECE = -(-(WINDOWS - 1 - EARLY) // LATE_PIECES)
        edge_sb = sb("edge_sb", [P, COLS], fp32)
        base_sb = sb("base_sb", [P, COLS], i32)
        rel_sb = base_sb[:, :].bitcast(fp32)
        win_row = sb("win_row", [1, G + COLS], i32)
        acc = [sb("acc", [P, WINDOWS, F + 1], fp32)[:, :, :], node_buf[:, :].rearrange("p (w f) -> p w f", f=F + 1)]
        b_table = sb("b_table", [P, WINDOWS, 3, F], bf16)

        stat = sb("stat", [P, 5, WINDOWS], fp32)
        viol = sb("viol", [P, CHECK_PIECES + 2], fp32)
        zero_col = sb("zero_col", [P, 1], fp32)
        flag = sb("flag", [1, 1], i32)
        counts = sb("counts", [P, 1], fp32)
        diag = sb("diag", [P, EXTRA], fp32)
        extra_tile = sb("extra_tile", [1, EXTRA], i32)
        extra_base = sb("extra_base", [P, EXTRA], fp32)

        idx = sb("idx", [P, SLOTS, G], i32)
        a_edge = sb("a_edge", [P, SLOTS, G, F], fp32)
        loop_buf = sb("loop_buf", [P, 3, SLOTS * G * F], fp32)
        ew, pre, rest = (loop_buf[:, n, :].rearrange("p (s g f) -> p s g f", s=SLOTS, g=G) for n in range(3))
        square = loop_buf[:, 0, 0:2 * GROUP * F].rearrange("p (s n) -> p s n", s=2)
        b_rest = loop_buf[:, 1:3, :].rearrange("p a n -> p (a n)")[:, 0:4 * GROUP * F].rearrange("p (s n) -> p s n", s=4)
        a_stage = b_rest
        hot_buf = sb("hot_buf", [P, 2, SLOTS, G, P], bf16)
        onehot, onehot_t = hot_buf[:, 0, :, :, :], hot_buf[:, 1, :, :, :]
        is_before = hot_buf[:, :, :, :, :].rearrange("p a s g n -> p (a s g n)")[:, 0:TILES]
        r_hi = sb("r_hi", [P, SLOTS, G, F + 1], bf16)
        r_mid = sb("r_mid", [P, SLOTS, G, F], bf16)
        r_lo = sb("r_lo", [P, SLOTS, G, F], bf16)

        check_a = acc[0].rearrange("p w f -> p (w f)")[0:CHECK_P, 0:CHECK_N + 1].bitcast(i32)
        check_d = b_table[:, :, :, :].rearrange("p w s f -> p (w s f)").bitcast(i32)[0:CHECK_P, 0:CHECK_N]
        h_t = x_sb[:, :, :].rearrange("p w f -> p (w f)").rearrange("p (k n) -> p k n", n=P)
        sums = b_table[:, :, :, :].rearrange("p w s f -> p (w s f)").bitcast(fp32)[:, 0:WINDOWS * F]
        less = b_table[:, :, :, :].rearrange("p w s f -> p (w s f)").bitcast(fp32)

        bank = [pb(f"bank{i}", [P, 512], fp32) for i in range(8)]
        EARLY_STEPS = [4, 7, 10]

        def bank_of_b(g):
            first = len(EARLY_STEPS)
            return bank[4 + g] if g < first else bank[(g - first) % 4]

        bank_t = [bank[s][:, 0:G * P // 2].bitcast(bf16).rearrange("p (g n) -> p g n", g=G) for s in range(3)]
        bank_b = [bank[3 + s][:, 0:G * F].rearrange("p (g f) -> p g f", g=G) for s in range(3)]
        bank_seg = bank[6][:, 0:G * (F + 1)].rearrange("p (g f) -> p g f", g=G)

        consts_loaded = sem("consts_loaded")
        weights_loaded = sem("weights_loaded")
        pads_set = sem("pads_set")
        setup_done = sem("setup_done")
        x_loaded = [sem(f"x_loaded{i}") for i in range(GROUPS)]
        x_early_loaded = sem("x_early_loaded")
        x_again_loaded = sem("x_again_loaded")
        flat_loaded = sem("flat_loaded")
        src_loaded = sem("src_loaded")
        dst_loaded = sem("dst_loaded")
        edge_loaded = sem("edge_loaded")
        base_loaded = sem("base_loaded")
        steps_ready = sem("steps_ready")
        least_ready = sem("least_ready")
        viol_ready = sem("viol_ready")
        edges_ordered = sem("edges_ordered")
        viol_summed = sem("viol_summed")
        flag_ready = sem("flag_ready")
        sum_ready = sem("sum_ready")
        mean_ready = sem("mean_ready")
        centred_ready = sem("centred_ready")
        squares_ready = sem("squares_ready")
        var_ready = sem("var_ready")
        inverse_ready = sem("inverse_ready")
        std_ready = sem("std_ready")
        h_ready = sem("h_ready")
        ht_in_psum = sem("ht_in_psum")
        ht_ready = sem("ht_ready")
        a_in_psum = sem("a_in_psum")
        a_staged = sem("a_staged")
        a_stored = [sem(f"a_stored{i}") for i in range(4)]
        b1_steps = sem("b1_steps")
        b_in_psum = sem("b_in_psum")
        b_upper_ready = sem("b_upper_ready")
        b_rest_ready = sem("b_rest_ready")
        b_middle_ready = sem("b_middle_ready")
        b_lower_ready = sem("b_lower_ready")
        prep_steps = sem("prep_steps")
        windows_ready = sem("windows_ready")
        win_row_ready = sem("win_row_ready")
        counts_ready = sem("counts_ready")
        counts_in_psum = sem("counts_in_psum")
        extra_tiles_ready = sem("extra_tiles_ready")
        tables_ready = sem("tables_ready")
        extra_cols_copied = [sem(f"extra_cols_copied{i}") for i in range(3)]
        first_idx_ready = sem("first_idx_ready")
        idx_loaded = [sem(f"idx_loaded{i}") for i in range(SLOTS)]
        a_gathered = [sem(f"a_gathered{i}") for i in range(SLOTS)]
        onehot_ready = sem("onehot_ready")
        onehot_t_in_psum = sem("onehot_t_in_psum")
        onehot_t_ready = sem("onehot_t_ready")
        b_expanded = sem("b_expanded")
        edge_terms_ready = sem("edge_terms_ready")
        a_added = sem("a_added")
        pre_ready = sem("pre_ready")
        r_hi_ready = sem("r_hi_ready")
        r_rest_ready = sem("r_rest_ready")
        r_mid_ready = sem("r_mid_ready")
        r_lo_ready = sem("r_lo_ready")
        sums_in_psum = sem("sums_in_psum")
        acc_steps = sem("acc_steps")
        sums_packed = sem("sums_packed")
        sums_t_in_psum = sem("sums_t_in_psum")
        sums_t_ready = sem("sums_t_ready")
        product_in_psum = sem("product_in_psum")
        out_ready = sem("out_ready")
        edges_counted = sem("edges_counted")
        bias_ready = sem("bias_ready")
        pool_bias_ready = sem("pool_bias_ready")
        x_biased = sem("x_biased")
        out_stored = sem("out_stored")
        below_counted = sem("below_counted")
        starts_in_psum = sem("starts_in_psum")
        sort_hot_ready = sem("sort_hot_ready")
        ranks_in_psum = sem("ranks_in_psum")
        sort_steps = sem("sort_steps")
        places_ready = sem("places_ready")
        scattered = [sem(f"scattered{i}") for i in range(SORT_SLOTS)]
        sorted_loaded = sem("sorted_loaded")

        sort_off = square[:, 0, 0:WINDOWS]
        sort_hot = square[:, 0, P:P + WINDOWS]
        sort_place = square[:, 0, 2 * P:2 * P + WINDOWS]
        sort_pick = square[:, 0, 3 * P:3 * P + WINDOWS]
        sort_winf = square[:, 1, 0:1]
        sort_posf = square[:, 1, 1:2]
        sort_posi = square[:, 1, 2:4].bitcast(i32)
        sort_posm = square[:, 1, 4:6].bitcast(i32)
        sort_posx = square[:, 1, 8:8 + SORT_SLOTS].bitcast(i32)
        sort_col_src = square[:, 1, 16:16 + SORT_SLOTS].bitcast(i32)
        sort_col_dst = square[:, 1, 24:24 + SORT_SLOTS].bitcast(i32)
        sort_col_edge = square[:, 1, 32:32 + SORT_SLOTS]

        def pool_sort(pool):
            placed = pool.alloc_register("placed")
            pool.reg_mov(placed, 1)
            with pool.Fori(0, SORT_TURNS) as turn:
                for slot in range(SORT_SLOTS):
                    pool.wait_ge(places_ready, placed)
                    pool.reg_alu(placed, placed, 1, ALU.add)
                    where = sort_posx[:, slot:slot + 1]
                    for table, col in ((sorted_src, sort_col_src), (sorted_dst, sort_col_dst), (sorted_edge, sort_col_edge)):
                        pool.indirect_dma_start(table, bass.IndirectOffsetOnAxis(where, 0), col[:, slot:slot + 1], None).then_inc(scattered[slot], 16)
            for slot in range(SORT_SLOTS):
                pool.wait_ge(scattered[slot], 16 * 3 * SORT_TURNS)
            cols = "(p t) o -> p (t o)"
            pool.dma_start(base_sb[:, 0:TILES], sorted_dst.rearrange(cols, p=P)[0:1, :].to_broadcast([P, TILES])).then_inc(sorted_loaded, 16)
            pool.dma_start(dst_sb[:, 0:TILES], sorted_dst.rearrange(cols, p=P)).then_inc(sorted_loaded, 16)
            pool.dma_start(src_sb[:, 0:TILES], sorted_src.rearrange(cols, p=P)).then_inc(sorted_loaded, 16)
            pool.dma_start(edge_sb[:, 0:TILES], sorted_edge.rearrange(cols, p=P)).then_inc(sorted_loaded, 16)

        def vector_sort(dve):
            dve.wait_ge(base_loaded, 16)
            dve.wait_ge(dst_loaded, 16)
            dve.wait_ge(src_loaded, 16)
            dve.wait_ge(edge_loaded, 16)
            nc.vector.memset(sort_place, 0.0).then_inc(below_counted, 1)
            dve.wait_ge(below_counted, 1)
            with dve.Fori(1, WINDOWS) as w:
                dve.wait_ge(below_counted, w * 2 - 1)
                nc.vector.tensor_scalar(sort_winf, iota[:, ds(w, 1)], float(P), None, ALU.mult).then_inc(below_counted, 1)
                dve.wait_ge(below_counted, w * 2)
                nc.vector.tensor_scalar(less[:, 0:TILES], dst_sb[:, 0:TILES], sort_winf, 0.0, ALU.is_lt, ALU.add,
                                        accum_out=sort_place[:, ds(w, 1)]).then_inc(below_counted, 1)
            dve.wait_ge(starts_in_psum, 1)
            nc.vector.tensor_copy(sort_off, bank[7][:, 0:WINDOWS]).then_inc(sort_steps, 1)
            dve.wait_ge(sort_steps, 1)
            nc.vector.tensor_scalar(less[:, 0:TILES].bitcast(i32), dst_sb[:, 0:TILES], 7, None, ALU.arith_shift_right).then_inc(sort_steps, 1)
            STEPS = 7

            def place_turn(turn, first):
                for slot in range(SORT_SLOTS):
                    tile = turn * SORT_SLOTS + slot
                    done = tile * STEPS + 2
                    dve.wait_ge(sort_steps, done)
                    nc.vector.tensor_copy(sort_winf, less[:, ds(tile, 1)].bitcast(i32)).then_inc(sort_steps, 1)
                    dve.wait_ge(sort_steps, done + 1)
                    nc.vector.tensor_scalar(sort_hot, iota[:, 0:WINDOWS], sort_winf, None, ALU.is_equal).then_inc(sort_hot_ready, 1)
                    dve.wait_ge(ranks_in_psum, tile + 1)
                    nc.vector.tensor_tensor(sort_pick, sort_off, bank[7][:, 0:WINDOWS], ALU.add).then_inc(sort_steps, 1)
                    dve.wait_ge(sort_steps, done + 2)
                    nc.vector.tensor_tensor(sort_pick, sort_pick, sort_hot, ALU.mult).then_inc(sort_steps, 1)
                    nc.vector.tensor_tensor(sort_off, sort_off, bank[7][:, P:P + WINDOWS], ALU.add)
                    dve.wait_ge(sort_steps, done + 3)
                    nc.vector.tensor_reduce(sort_posf, sort_pick, AX.X, ALU.add).then_inc(sort_steps, 1)
                    dve.wait_ge(sort_steps, done + 4)
                    nc.vector.tensor_copy(sort_posi[:, 0:1], sort_posf).then_inc(sort_steps, 1)
                    dve.wait_ge(sort_steps, done + 5)
                    nc.vector.tensor_scalar(sort_posi[:, 1:2], sort_posi[:, 0:1], 7, None, ALU.arith_shift_right)
                    nc.vector.tensor_scalar(sort_posm[:, 0:1], sort_posi[:, 0:1], P - 1, None, ALU.bitwise_and).then_inc(sort_steps, 1)
                    dve.wait_ge(sort_steps, done + 6)
                    if not first:
                        dve.wait_ge(scattered[slot], turn * (16 * 3))
                    nc.vector.scalar_tensor_tensor(sort_posx[:, slot:slot + 1], sort_posm[:, 0:1], float(TILES), sort_posi[:, 1:2], ALU.mult, ALU.add).then_inc(sort_steps, 1)
                    nc.vector.tensor_copy(sort_col_src[:, slot:slot + 1], src_sb[:, ds(tile, 1)])
                    nc.vector.tensor_copy(sort_col_dst[:, slot:slot + 1], dst_sb[:, ds(tile, 1)])
                    dve.wait_ge(sort_steps, done + 7)
                    nc.vector.tensor_copy(sort_col_edge[:, slot:slot + 1], edge_sb[:, ds(tile, 1)]).then_inc(places_ready, 1)

            place_turn(0, True)
            with dve.Fori(1, SORT_TURNS) as turn:
                place_turn(turn, False)
            dve.wait_ge(sorted_loaded, 16 * 4)

        def tensor_sort(pe):
            pe.wait_ge(below_counted, 2 * WINDOWS - 1)
            nc.tensor.matmul(bank[7][:, 0:WINDOWS], ones[:, :], sort_place, start=True, stop=True).then_inc(starts_in_psum, 1)
            pe.wait_ge(sort_steps, 1)
            with pe.Fori(0, TILES) as tile:
                pe.wait_ge(sort_hot_ready, tile + 1)
                nc.tensor.matmul(bank[7][:, 0:WINDOWS], before, sort_hot, start=True, stop=True)
                nc.tensor.matmul(bank[7][:, P:P + WINDOWS], ones[:, :], sort_hot, start=True, stop=True).then_inc(ranks_in_psum, 1)

        WINDOW_STEP, COUNT_STEP, REL_STEP, EXTRA_STEP, EDGE_STEP = 4, 6, 8, 9, 11

        def load_windows(eng, regs, first):
            eng.reg_load(regs, win_row[0:1, ds(first, G)])
            return [eng.snap(r, min_val=0, max_val=WINDOWS - 1) for r in regs]

        POOL_BIAS = GROUPS - 5

        def bias_of(g):
            return b_rest[:, g % 4, 0:group_windows(g) * F].rearrange("p (w f) -> p w f", f=F)

        def edge_bias(eng, g):
            n = group_windows(g)
            return eng.tensor_tensor(bias_of(g), acc[0][:, g * GROUP:g * GROUP + n, F:F + 1].to_broadcast([P, n, F]),
                                     b2_rows[:, :].unsqueeze(1).to_broadcast([P, n, F]), ALU.mult)

        def a_rows_out(eng, slot):
            eng.wait_ge(a_stored[slot], 16 * len(range(slot, GROUPS, 4)))

        def a_table_done(eng):
            for slot in range(4):
                a_rows_out(eng, slot)

        block = ctx.enter_context(nc.Block())

        @block.sync
        def _(sp):
            sp.dma_start(cst[:, :], consts).then_inc(consts_loaded, 16)
            full = x[0:(WINDOWS - 1) * P, :].rearrange("(w p) f -> p w f", p=P)
            corners = [slice(k * F, (k + 1) * F) for k in range(2)]
            weights = [(w1a[c, c], w1[0:F, :]) for c in corners]
            weights += [(b1_rows[:, :], b1.unsqueeze(0).to_broadcast([P, F]))]
            weights += [(w1b[c, c], w1[F:2 * F, :]) for c in corners]
            weights += [(w2d[c, c], w2) for c in corners]
            weights += [(we_rows[:, :], w1[2 * F:2 * F + 1, :].to_broadcast([P, F])), (b2_rows[:, :], b2.unsqueeze(0).to_broadcast([P, F]))]
            for g in range(GROUPS):
                n = group_windows(g)
                if 1 <= g <= len(weights):
                    if g == 1:
                        sp.wait_ge(setup_done, 1)
                    sp.dma_start(*weights[g - 1]).then_inc(weights_loaded, 16)
                if g == GROUPS - 1:
                    sp.wait_ge(setup_done, 1)
                    sp.dma_start(x_sb[:, g * GROUP:WINDOWS - 1, :], full[:, g * GROUP:WINDOWS - 1, :]).then_inc(x_loaded[g], 16)
                    sp.dma_start(x_sb[0:TAIL, WINDOWS - 1, :], x[(WINDOWS - 1) * P:NODES, :]).then_inc(x_loaded[g], 16)
                else:
                    sp.dma_start(x_sb[:, g * GROUP:g * GROUP + n, :], full[:, g * GROUP:g * GROUP + n, :]).then_inc(x_loaded[g], 16)
            rows = dst_flat.rearrange("(p n) -> p n", p=CHECK_P)
            sp.dma_start(check_a[:, 0:CHECK_N], rows).then_inc(flat_loaded, 16)
            with nc.allow_non_contiguous_dma("one value a row"):
                sp.dma_start(check_a[0:CHECK_P - 1, CHECK_N:CHECK_N + 1], rows[1:CHECK_P, 0:1]).then_inc(flat_loaded, 16)
            for g in range(GROUPS):
                n = group_windows(g)
                sp.wait_ge(a_staged, g + 1)
                sp.dma_start(a_rows[:, g * GROUP:g * GROUP + n, :],
                             a_stage[:, g % 4, 0:n * F].rearrange("p (w f) -> p w f", f=F)).then_inc(a_stored[g % 4], 16)
                if g == 3:
                    sp.dma_start(src_sb[:, 0:TILES], src_cols).then_inc(src_loaded, 16)
            sp.dma_start(base_sb[:, 0:TILES], dst_cols[0:1, :].to_broadcast([P, TILES])).then_inc(base_loaded, 16)
            sp.dma_start(dst_sb[:, 0:TILES], dst_cols).then_inc(dst_loaded, 16)
            sp.dma_start(edge_sb[:, 0:TILES], edge_cols).then_inc(edge_loaded, 16)

            def load_turn(turn):
                for slot in range(SLOTS):
                    sp.wait_ge(a_gathered[slot], turn * (16 * G))
                    sp.dma_start(idx[:, slot, :], src_sb[:, ds((turn * SLOTS + slot) * G, G)]).then_inc(idx_loaded[slot], 16)

            sp.wait_ge(extra_tiles_ready, 1)
            sp.wait_ge(dst_loaded, 16)
            sp.wait_ge(edge_loaded, 16)
            with sp.Fori(1, EXTRA + 1) as turn:
                load_turn(turn)
                tile = sp.value_load(extra_tile[0:1, ds(turn - 1, 1)], min_val=0, max_val=TILES - 1)
                with nc.allow_non_contiguous_dma("one column of four-byte values"):
                    for n, cols in enumerate((src_sb, dst_sb, edge_sb)):
                        sp.dma_start(cols[:, ds(turn + (TILES - 1), 1)], cols[:, ds(tile, 1)]).then_inc(extra_cols_copied[n], 16)
            for n in range(3):
                sp.wait_ge(extra_cols_copied[n], 16 * EXTRA)
            with sp.Fori(EXTRA + 1, TILE_TURNS + 1) as turn:
                load_turn(turn)

            sp.wait_ge(tables_ready, 2)
            with sp.Fori(TILE_TURNS + 1, TURNS) as turn:
                load_turn(turn)
                piece = ds((turn - (TILE_TURNS + 1)) * EARLY_PIECE, EARLY_PIECE)
                sp.dma_start(x_again[:, piece, :], full[:, piece, :]).then_inc(x_early_loaded, 16)
            for slot in range(SLOTS):
                sp.wait_ge(idx_loaded[slot], 16 * (TURNS - 1))
            for k in range(LATE_PIECES):
                w = slice(EARLY + k * LATE_PIECE, min(EARLY + (k + 1) * LATE_PIECE, WINDOWS - 1))
                if k >= 1:
                    sp.wait_ge(x_again_loaded, 16 * k)
                sp.dma_start(x_again[:, w, :], full[:, w, :]).then_inc(x_again_loaded, 16)
            sp.dma_start(x_again[0:TAIL, WINDOWS - 1, :], x[(WINDOWS - 1) * P:NODES, :]).then_inc(x_again_loaded, 16)
            for g in range(GROUPS):
                n = group_windows(g)
                sp.wait_ge(out_ready, g + 1)
                last = g == GROUPS - 1
                m = n - 1 if last else n
                if m:
                    sp.dma_start(out[g * GROUP * P:(g * GROUP + m) * P, :].rearrange("(w p) f -> p w f", p=P),
                                 x_again[:, g * GROUP:g * GROUP + m, :]).then_inc(out_stored, 16)
                if last:
                    sp.dma_start(out[(WINDOWS - 1) * P:NODES, :], x_again[0:TAIL, WINDOWS - 1, :]).then_inc(out_stored, 16)
            sp.wait_ge(out_stored, 16 * (GROUPS + 1))

        @block.scalar
        def _(act):
            for step in range(GROUPS + 4):
                if step < GROUPS:
                    g, n = step, group_windows(step)
                    act.wait_ge(centred_ready, g + 1)
                    if g >= 2:
                        act.wait_ge(var_ready, g - 1)
                    nc.scalar.activation(square[:, g % 2, 0:n * F], x_sb[:, g * GROUP:g * GROUP + n, :].rearrange("p w f -> p (w f)"),
                                         ACT.Square).then_inc(squares_ready, 1)
                if 1 <= step <= GROUPS:
                    g, n = step - 1, group_windows(step - 1)
                    w = slice(g * GROUP, g * GROUP + n)
                    act.wait_ge(var_ready, g + 1)
                    nc.scalar.activation(stat[:, 3, w], stat[:, 2, w], ACT.Sqrt, bias=eps_col[:, :], scale=1.0 / F).then_inc(std_ready, 1)
                if 3 <= step < GROUPS + 3:
                    g, n = step - 3, group_windows(step - 3)
                    act.wait_ge(ht_in_psum, g + 1)
                    nc.scalar.copy(h_t[:, g * 4:g * 4 + n // 2, :].rearrange("p k n -> p (k n)"), bank[g % 2][:, 0:n * F]).then_inc(ht_ready, 1)
                if 4 <= step:
                    g, n = step - 4, group_windows(step - 4)
                    act.wait_ge(a_in_psum, g + 1)
                    if g >= 4:
                        act.wait_ge(a_stored[g % 4], 16 * (g // 4))
                    nc.scalar.copy(a_stage[:, g % 4, 0:n * F], bank[2 + g % 2][:, 0:n * F]).then_inc(a_staged, 1)
            act.wait_ge(edges_ordered, 1)
            for step in range(GROUPS + 1):
                if step < GROUPS:
                    g, n = step, group_windows(step)
                    act.wait_ge(b_in_psum, g + 1)
                    nc.scalar.copy(b_table[:, g * GROUP:g * GROUP + n, 0, :], bank_of_b(g)[:, 0:n * F].rearrange("p (w f) -> p w f", f=F)).then_inc(b_upper_ready, 1)
                    if g >= len(EARLY_STEPS):
                        cells = slice(g * GROUP * F, (g + 1) * GROUP * F if g < GROUPS - 1 else WINDOWS * (F + 1))
                        size = cells.stop - cells.start
                        last = nc.scalar.copy(node_buf[:, cells], zero_col[:, :].to_broadcast([P, size]))
                if step == REL_STEP:
                    act.wait_ge(b_rest_ready, 3)
                    nc.scalar.copy(bank_seg, zero_col[:, :].unsqueeze(1).to_broadcast([P, G, F + 1])).then_inc(sums_in_psum, 1)
                if step == COUNT_STEP:
                    act.wait_ge(windows_ready, 1)
                    act.dma_start(win_row[0:1, G:G + TILES], base_sb[0:1, 0:TILES]).then_inc(win_row_ready, 16)
                if step >= 1:
                    g, n = step - 1, group_windows(step - 1)
                    act.wait_ge(b_rest_ready, g + 1)
                    nc.scalar.copy(b_table[:, g * GROUP:g * GROUP + n, 1, :], b_rest[:, (g + 1) % 4, 0:n * F].rearrange("p (w f) -> p w f", f=F)).then_inc(b_middle_ready, 1)
            last.then_inc(acc_steps, 1)

            def one_hot_out(batch, slot):
                act.wait_ge(onehot_t_in_psum, batch + 1)
                nc.scalar.copy(onehot_t[:, slot, :, :], bank_t[slot]).then_inc(onehot_t_ready, 1)

            act.wait_ge(tables_ready, 1)
            one_hot_out(0, 0)
            with act.Fori(0, TURNS) as turn:
                for slot in range(SLOTS):
                    batch = turn * SLOTS + slot
                    act.wait_ge(pre_ready, batch + 1)
                    nc.scalar.activation(r_hi[:, slot, :, 0:F], pre[:, slot, :, :], ACT.Relu).then_inc(r_hi_ready, 1)
                    one_hot_out(batch + 1, (slot + 1) % SLOTS)
                    act.wait_ge(r_rest_ready, batch + 1)
                    nc.scalar.copy(r_mid[:, slot, :, :], rest[:, slot, :, :]).then_inc(r_mid_ready, 1)
            for g in range(GROUPS):
                n = group_windows(g)
                act.wait_ge(sums_t_in_psum, g + 1)
                nc.scalar.copy(sums[:, g * GROUP * F:(g * GROUP + n) * F], bank[g % 2][:, 0:n * F]).then_inc(sums_t_ready, 1)

        @block.gpsimd
        def _(pool):
            nc.gpsimd.memset(x_sb[F:P, WINDOWS - 1, :], 0.0).then_inc(pads_set, 1)
            pool.wait_ge(pads_set, 1)
            nc.gpsimd.memset(check_a[96:CHECK_P, CHECK_N:CHECK_N + 1], NODES).then_inc(pads_set, 1)
            pool.wait_ge(pads_set, 2)
            nc.gpsimd.memset(w1a[:, :], 0.0)
            nc.gpsimd.memset(w1b[:, :], 0.0)
            nc.gpsimd.memset(w2d[:, :], 0.0)
            nc.gpsimd.memset(eps_col[:, :], EPS)
            nc.gpsimd.memset(zero_col[:, :], 0.0)
            nc.gpsimd.memset(viol[:, :], 0.0)
            nc.gpsimd.memset(ones[:, :], 1.0).then_inc(setup_done, 1)
            pool.wait_ge(consts_loaded, 16)
            nc.gpsimd.memset(ones_bf[:, :], 1.0)
            nc.gpsimd.tensor_copy(ident_bf[:, :], ident).then_inc(setup_done, 1)
            for g in range(GROUPS):
                n = group_windows(g)
                w = slice(g * GROUP, g * GROUP + n)
                pool.wait_ge(mean_ready, g + 1)
                nc.gpsimd.tensor_tensor(x_sb[:, w, :], x_sb[:, w, :], stat[:, 1, w].unsqueeze(2).to_broadcast([P, n, F]), ALU.subtract).then_inc(centred_ready, 1)
                k = g - (GROUPS - CHECK_PIECES)
                if k >= 0:
                    c = slice(k * PIECE, (k + 1) * PIECE)
                    pool.wait_ge(flat_loaded, 32)
                    nc.gpsimd.tensor_tensor(check_d[:, c], check_a[:, k * PIECE + 1:(k + 1) * PIECE + 1], check_a[:, c], ALU.subtract).then_inc(steps_ready, 1)
            pool.wait_ge(steps_ready, CHECK_PIECES)
            nc.gpsimd.memset(acc[0], 0.0)
            pool.wait_ge(b_in_psum, len(EARLY_STEPS))
            nc.gpsimd.memset(node_buf[:, 0:len(EARLY_STEPS) * GROUP * F], 0.0).then_inc(acc_steps, 1)
            pool.wait_ge(flag_ready, 1)
            unsorted = pool.value_load(flag[0:1, 0:1], min_val=0, max_val=1)
            with pool.If(unsorted):
                pool_sort(pool)
            pool.wait_ge(src_loaded, 16)
            pool.wait_ge(edges_ordered, 1)
            nc.gpsimd.tensor_copy(idx[:, :, :].rearrange("p s g -> p (s g)"), src_sb[:, 0:SLOTS * G]).then_inc(first_idx_ready, 1)
            pool.wait_ge(first_idx_ready, 1)
            a_table_done(pool)
            used = pool.alloc_register("used")
            pool.reg_mov(used, 1)

            def gather(turn, slot, first):
                if not first:
                    pool.wait_ge(idx_loaded[slot], turn * 16)
                    pool.wait_ge(a_added, used)
                    pool.reg_alu(used, used, 1, ALU.add)
                for v in range(G):
                    pool.indirect_dma_start(a_edge[:, slot, v, :], None, a_table,
                                            bass.IndirectOffsetOnAxis(idx[:, slot, v:v + 1], 0)).then_inc(a_gathered[slot], 16)

            for slot in range(SLOTS):
                gather(0, slot, True)
            with pool.Fori(1, TURNS) as turn:
                for slot in range(SLOTS):
                    gather(turn, slot, False)
            pool.wait_ge(acc_steps, G * (BATCHES + 1) + 2)
            for g in range(GROUPS):
                n = group_windows(g)
                w = slice(g * GROUP, g * GROUP + n)
                nc.gpsimd.tensor_tensor(sums[:, g * GROUP * F:(g * GROUP + n) * F].rearrange("p (w f) -> p w f", f=F), acc[0][:, w, 0:F], acc[1][:, w, 0:F], ALU.add).then_inc(sums_packed, 1)
            pool.wait_ge(edges_counted, 1)
            for g in range(POOL_BIAS, GROUPS):
                pool.wait_ge(x_biased, g - 3)
                edge_bias(nc.gpsimd, g).then_inc(pool_bias_ready, 1)

        @block.vector
        def _(dve):
            for step in range(GROUPS + 2):
                if step < GROUPS:
                    g, n = step, group_windows(step)
                    w = slice(g * GROUP, g * GROUP + n)
                    dve.wait_ge(x_loaded[g], 16 if g < GROUPS - 1 else 32)
                    nc.vector.tensor_reduce(stat[:, 0, w], x_sb[:, w, :], AX.X, ALU.add).then_inc(sum_ready, 1)
                    dve.wait_ge(sum_ready, g + 1)
                    nc.vector.tensor_scalar(stat[:, 1, w], stat[:, 0, w], 1.0 / F, None, ALU.mult).then_inc(mean_ready, 1)
                if 1 <= step <= GROUPS:
                    g, n = step - 1, group_windows(step - 1)
                    w = slice(g * GROUP, g * GROUP + n)
                    dve.wait_ge(squares_ready, g + 1)
                    nc.vector.tensor_reduce(stat[:, 2, w], square[:, g % 2, 0:n * F].rearrange("p (w f) -> p w f", f=F), AX.X, ALU.add).then_inc(var_ready, 1)
                if step >= 2:
                    g, n = step - 2, group_windows(step - 2)
                    w = slice(g * GROUP, g * GROUP + n)
                    dve.wait_ge(std_ready, g + 1)
                    nc.vector.reciprocal(stat[:, 4, w], stat[:, 3, w]).then_inc(inverse_ready, 1)
                    dve.wait_ge(inverse_ready, g + 1)
                    nc.vector.scalar_tensor_tensor(x_sb[:, w, :], x_sb[:, w, :], 0.0, stat[:, 4, w].unsqueeze(2).to_broadcast([P, n, F]),
                                                   ALU.max, ALU.mult).then_inc(h_ready, 1)
                if step == EARLY_STEPS[0]:
                    dve.wait_ge(weights_loaded, 16 * 9)
                    dve.wait_ge(consts_loaded, 16)
                    nc.vector.tensor_copy(b1_bf[:, 0, :], b1_rows[:, :]).then_inc(b1_steps, 1)
                    dve.wait_ge(b1_steps, 1)
                    nc.vector.tensor_tensor(b1_part[:, 1, :], b1_rows[:, :], b1_bf[:, 0, :], ALU.subtract).then_inc(b1_steps, 1)
                    nc.vector.tensor_scalar(b1_part[:, 0, :], b1_bf[:, 0, :], ident[:, 0:1], None, ALU.mult).then_inc(b1_steps, 1)
                    dve.wait_ge(b1_steps, 2)
                    nc.vector.tensor_copy(b1_bf[:, 1, :], b1_part[:, 1, :]).then_inc(b1_steps, 1)
                    dve.wait_ge(b1_steps, 4)
                    nc.vector.tensor_tensor(b1_part[:, 2, :], b1_part[:, 1, :], b1_bf[:, 1, :], ALU.subtract).then_inc(b1_steps, 1)
                    nc.vector.scalar_tensor_tensor(b1_part[:, 0, :], b1_bf[:, 1, :], ident[:, 1:2], b1_part[:, 0, :], ALU.mult, ALU.add).then_inc(b1_steps, 1)
                    dve.wait_ge(b1_steps, 6)
                    nc.vector.scalar_tensor_tensor(b1_split[:, :], b1_part[:, 2, :], ident[:, 2:3], b1_part[:, 0, :], ALU.mult, ALU.add).then_inc(b1_steps, 1)
                k = step - (GROUPS + 2 - CHECK_PIECES)
                if k >= 0:
                    dve.wait_ge(steps_ready, k + 1)
                    nc.vector.tensor_reduce(viol[0:CHECK_P, 2 + k:3 + k], check_d[:, k * PIECE:(k + 1) * PIECE], AX.X, ALU.min).then_inc(least_ready, 1)

            dve.wait_ge(least_ready, CHECK_PIECES)
            dve.wait_ge(setup_done, 2)
            nc.vector.tensor_reduce(viol[0:CHECK_P, 1:2], viol[0:CHECK_P, 2:2 + CHECK_PIECES], AX.X, ALU.min).then_inc(viol_ready, 1)
            dve.wait_ge(viol_ready, 1)
            nc.vector.tensor_scalar(viol[0:CHECK_P, 0:1], viol[0:CHECK_P, 1:2], 0.0, None, ALU.is_lt).then_inc(viol_ready, 1)
            dve.wait_ge(viol_summed, 1)
            nc.vector.tensor_scalar(flag[0:1, 0:1], bank[7][0:1, 0:1], 1.0, None, ALU.min).then_inc(flag_ready, 1)
            nc.vector.memset(win_row[:, 0:G], 0)
            nc.vector.memset(win_row[:, G + VISITS:G + COLS], 0)
            nc.vector.tensor_copy(win_row[0:1, G + TILES:G + VISITS], iota[0:1, 1:WINDOWS])
            dve.wait_ge(flag_ready, 1)
            unsorted = dve.value_load(flag[0:1, 0:1], min_val=0, max_val=1)
            with dve.If(unsorted):
                vector_sort(dve)
            nc.vector.memset(edge_sb[:, VISITS:COLS], 0.0).then_inc(edges_ordered, 1)
            FIRST_COLS = (SLOTS + 1) * G

            def relative_dst(first, last):
                c = slice(first, last)
                nc.vector.scalar_tensor_tensor(rel_sb[:, c], base_sb[:, c], -float(P), dst_sb[:, c], ALU.mult, ALU.add).then_inc(prep_steps, 1)

            def one_hots(batch, slot):
                nc.vector.tensor_tensor(onehot[:, slot, :, :], rel_sb[:, ds(batch * G, G)].unsqueeze(2).to_broadcast([P, G, P]),
                                        iota.unsqueeze(1).to_broadcast([P, G, P]), ALU.is_equal).then_inc(onehot_ready, 1)

            def edge_terms(batch, slot):
                nc.vector.tensor_tensor(ew[:, slot, :, :], edge_sb[:, ds(batch * G, G)].unsqueeze(2).to_broadcast([P, G, F]),
                                        we_rows[:, :].unsqueeze(1).to_broadcast([P, G, F]), ALU.mult).then_inc(edge_terms_ready, 1)

            for step in range(GROUPS + 1):
                if step < GROUPS:
                    g, n = step, group_windows(step)
                    w = slice(g * GROUP, g * GROUP + n)
                    dve.wait_ge(b_upper_ready, g + 1)
                    if g >= 4:
                        dve.wait_ge(b_lower_ready, g - 3)
                    else:
                        a_rows_out(dve, (g + 1) % 4)
                    nc.vector.tensor_tensor(b_rest[:, (g + 1) % 4, 0:n * F].rearrange("p (w f) -> p w f", f=F),
                                            bank_of_b(g)[:, 0:n * F].rearrange("p (w f) -> p w f", f=F), b_table[:, w, 0, :], ALU.subtract).then_inc(b_rest_ready, 1)
                if step >= 1:
                    g, n = step - 1, group_windows(step - 1)
                    w = slice(g * GROUP, g * GROUP + n)
                    dve.wait_ge(b_middle_ready, g + 1)
                    nc.vector.tensor_tensor(b_table[:, w, 2, :], b_rest[:, (g + 1) % 4, 0:n * F].rearrange("p (w f) -> p w f", f=F),
                                            b_table[:, w, 1, :], ALU.subtract).then_inc(b_lower_ready, 1)
                if step == WINDOW_STEP:
                    dve.wait_ge(base_loaded, 16)
                    nc.vector.tensor_scalar(base_sb[:, 0:TILES], base_sb[:, 0:TILES], 7, None, ALU.arith_shift_right).then_inc(windows_ready, 1)
                if step == COUNT_STEP:
                    dve.wait_ge(windows_ready, 1)
                    nc.vector.tensor_scalar(is_before[0:EXTRA, :], base_sb[0:EXTRA, 0:TILES], next_window[0:EXTRA, :], 0.0,
                                            ALU.is_lt, ALU.add, accum_out=counts[0:EXTRA, :]).then_inc(prep_steps, 1)
                    dve.wait_ge(prep_steps, 1)
                    nc.vector.tensor_scalar(diag[0:EXTRA, :], ident[0:EXTRA, 0:EXTRA], counts[0:EXTRA, :], None, ALU.mult).then_inc(counts_ready, 1)
                if step == REL_STEP:
                    dve.wait_ge(win_row_ready, 16)
                    dve.wait_ge(dst_loaded, 16)
                    relative_dst(0, FIRST_COLS)
                    nc.vector.memset(rel_sb[:, VISITS:COLS], -1.0).then_inc(prep_steps, 1)
                    dve.wait_ge(prep_steps, 3)
                    one_hots(0, 0)
                if step == EXTRA_STEP:
                    dve.wait_ge(counts_in_psum, 1)
                    nc.vector.tensor_scalar(extra_tile[0:1, :], bank[7][0:1, 0:EXTRA], -1.0, 0.0, ALU.add, ALU.max).then_inc(extra_tiles_ready, 1)
                    nc.vector.tensor_scalar(extra_base[:, :], bank[7][:, 0:EXTRA], 0.0, FAR, ALU.is_equal, ALU.mult).then_inc(prep_steps, 1)
                    dve.wait_ge(prep_steps, 4)
                    nc.vector.scalar_tensor_tensor(extra_base[:, :], iota[:, 1:WINDOWS], float(P), extra_base[:, :], ALU.mult, ALU.add).then_inc(prep_steps, 1)
                if step == EDGE_STEP:
                    dve.wait_ge(edge_loaded, 16)
                    edge_terms(0, 0)
                    nc.vector.memset(r_hi[:, :, :, F:F + 1], 1.0).then_inc(tables_ready, 1)
            dve.wait_ge(acc_steps, 2)
            dve.wait_ge(b_lower_ready, GROUPS)

            window_regs = [dve.alloc_register(f"dve_window{v}") for v in range(G)]

            def accumulate(batch, windows, visits):
                for v in visits:
                    if v == 0:
                        dve.wait_ge(sums_in_psum, batch + 1)
                    dve.wait_ge(acc_steps, batch * G + (v + 1))
                    here = acc[v % 2][:, ds(windows[v], 1), :].rearrange("p w f -> p (w f)")
                    nc.vector.tensor_tensor(here, here, bank_seg[:, v, :], ALU.add).then_inc(acc_steps, 1)

            def turn_of_batches(turn):
                for slot in range(SLOTS):
                    batch = turn * SLOTS + slot
                    after = (slot + 1) % SLOTS
                    windows = load_windows(dve, window_regs, batch * G)
                    one_hots(batch + 1, after)
                    dve.wait_ge(edge_terms_ready, batch + 1)
                    dve.wait_ge(a_gathered[slot], (turn + 1) * (16 * G))
                    nc.vector.tensor_tensor(pre[:, slot, :, :], ew[:, slot, :, :], a_edge[:, slot, :, :], ALU.add).then_inc(a_added, 1)
                    dve.wait_ge(a_added, batch + 1)
                    dve.wait_ge(b_expanded, batch + 1)
                    nc.vector.tensor_tensor(pre[:, slot, :, :], pre[:, slot, :, :], bank_b[slot], ALU.add).then_inc(pre_ready, 1)
                    accumulate(batch, windows, range(0, G // 2))
                    edge_terms(batch + 1, after)
                    dve.wait_ge(r_hi_ready, batch + 1)
                    nc.vector.scalar_tensor_tensor(rest[:, slot, :, :], pre[:, slot, :, :], 0.0, r_hi[:, slot, :, 0:F],
                                                   ALU.max, ALU.subtract).then_inc(r_rest_ready, 1)
                    accumulate(batch, windows, range(G // 2, G))
                    dve.wait_ge(r_mid_ready, batch + 1)
                    nc.vector.tensor_tensor(r_lo[:, slot, :, :], rest[:, slot, :, :], r_mid[:, slot, :, :], ALU.subtract).then_inc(r_lo_ready, 1)

            turn_of_batches(0)
            relative_dst(FIRST_COLS, TILES)
            dve.wait_ge(prep_steps, 6)
            with dve.Fori(1, TILE_TURNS) as turn:
                turn_of_batches(turn)
            for n in range(3):
                dve.wait_ge(extra_cols_copied[n], 16 * EXTRA)
            nc.vector.tensor_tensor(rel_sb[:, TILES:VISITS], dst_sb[:, TILES:VISITS], extra_base[:, :], ALU.subtract).then_inc(tables_ready, 1)
            dve.wait_ge(tables_ready, 2)
            with dve.Fori(TILE_TURNS, TURNS) as turn:
                turn_of_batches(turn)
            accumulate(BATCHES, load_windows(dve, window_regs, BATCHES * G), range(G))

            dve.wait_ge(acc_steps, G * (BATCHES + 1) + 2)
            edges = acc[0][:, :, F:F + 1]
            nc.vector.tensor_tensor(edges, edges, acc[1][:, :, F:F + 1], ALU.add).then_inc(edges_counted, 1)
            dve.wait_ge(edges_counted, 1)
            dve.wait_ge(x_early_loaded, 16 * (TURNS - TILE_TURNS - 1))
            dve.wait_ge(x_again_loaded, 16 * (LATE_PIECES + 1))
            for step in range(GROUPS + 2):
                if step < GROUPS:
                    g, n = step, group_windows(step)
                    w = slice(g * GROUP, g * GROUP + n)
                    if g < POOL_BIAS:
                        if g >= 4:
                            dve.wait_ge(x_biased, g - 3)
                        edge_bias(nc.vector, g).then_inc(bias_ready, 1)
                        dve.wait_ge(bias_ready, g + 1)
                    else:
                        dve.wait_ge(pool_bias_ready, g - POOL_BIAS + 1)
                    nc.vector.tensor_tensor(x_again[:, w, :], x_again[:, w, :], bias_of(g), ALU.add).then_inc(x_biased, 1)
                if step >= 2:
                    g, n = step - 2, group_windows(step - 2)
                    w = slice(g * GROUP, g * GROUP + n)
                    dve.wait_ge(x_biased, g + 1)
                    dve.wait_ge(product_in_psum, g + 1)
                    nc.vector.tensor_tensor(x_again[:, w, :], x_again[:, w, :], bank[2 + g % 2][:, 0:n * F].rearrange("p (w f) -> p w f", f=F), ALU.add).then_inc(out_ready, 1)

        @block.tensor
        def _(pe):
            def b_group(g):
                n = group_windows(g)
                nc.tensor.matmul(bank_of_b(g)[:, 0:n * F], ones_bf[:, :], b1_split[:, :].unsqueeze(1).to_broadcast([P, n, F]), start=True, stop=False)
                for k in range(n // 2):
                    last = nc.tensor.matmul(bank_of_b(g)[:, k * P:(k + 1) * P], h_t[:, g * 4 + k, :], w1b[:, :], start=False, stop=k == n // 2 - 1)
                last.then_inc(b_in_psum, 1)

            pe.wait_ge(setup_done, 2)
            pe.wait_ge(weights_loaded, 16 * 9)
            for step in range(GROUPS + 1):
                if step < GROUPS:
                    g, n = step, group_windows(step)
                    pe.wait_ge(h_ready, g + 1)
                    if g >= 2:
                        pe.wait_ge(ht_ready, g - 1)
                    for k in range(n // 2):
                        w = g * GROUP + 2 * k
                        last = nc.tensor.transpose(bank[g % 2][:, k * P:(k + 1) * P], x_sb[:, w:w + 2, :].rearrange("p w f -> p (w f)"), ident)
                    last.then_inc(ht_in_psum, 1)
                if step >= 1:
                    g, n = step - 1, group_windows(step - 1)
                    pe.wait_ge(ht_ready, g + 1)
                    if g >= 2:
                        pe.wait_ge(a_staged, g - 1)
                    for k in range(n // 2):
                        last = nc.tensor.matmul(bank[2 + g % 2][:, k * P:(k + 1) * P], h_t[:, g * 4 + k, :], w1a[:, :], start=True, stop=True)
                    last.then_inc(a_in_psum, 1)
                if step in EARLY_STEPS:
                    if step == EARLY_STEPS[0]:
                        pe.wait_ge(b1_steps, 7)
                    b_group(EARLY_STEPS.index(step))
            pe.wait_ge(viol_ready, 2)
            nc.tensor.matmul(bank[7][:, 0:1], ones[:, :], viol[:, 0:1], start=True, stop=True).then_inc(viol_summed, 1)
            pe.wait_ge(flag_ready, 1)
            unsorted = pe.value_load(flag[0:1, 0:1], min_val=0, max_val=1)
            with pe.If(unsorted):
                tensor_sort(pe)
            pe.wait_ge(ht_ready, GROUPS)
            pe.wait_ge(a_staged, GROUPS)
            for g in range(len(EARLY_STEPS), GROUPS):
                if g >= len(EARLY_STEPS) + 4:
                    pe.wait_ge(b_rest_ready, g - 3)
                b_group(g)
                if g == EXTRA_STEP:
                    pe.wait_ge(counts_ready, 1)
                    nc.tensor.matmul(bank[7][:, 0:EXTRA], ones[0:EXTRA, :], diag[0:EXTRA, :], start=True, stop=True).then_inc(counts_in_psum, 1)
            def transposes(batch, slot):
                pe.wait_ge(onehot_ready, batch + 1)
                for v in range(G):
                    last = nc.tensor.transpose(bank_t[slot][:, v, :], onehot[:, slot, v, :], ident_bf[:, :])
                last.then_inc(onehot_t_in_psum, 1)

            def expand(batch, slot, windows):
                pe.wait_ge(onehot_t_ready, batch + 1)
                for v in range(G):
                    for part in range(3):
                        last = nc.tensor.matmul(bank_b[slot][:, v, :], onehot_t[:, slot, v, :],
                                                b_table[:, ds(windows[v], 1), part, :].rearrange("p w f -> p (w f)"),
                                                start=part == 0, stop=part == 2)
                last.then_inc(b_expanded, 1)

            window_regs = [pe.alloc_register(f"pe_window{v}") for v in range(G)]

            pe.wait_ge(b_rest_ready, GROUPS)
            transposes(0, 0)
            pe.wait_ge(win_row_ready, 16)
            windows = load_windows(pe, window_regs, G)
            pe.wait_ge(b_lower_ready, GROUPS)
            expand(0, 0, windows)
            pe.wait_ge(tables_ready, 1)
            with pe.Fori(0, TURNS) as turn:
                for slot in range(SLOTS):
                    batch = turn * SLOTS + slot
                    after = (slot + 1) % SLOTS
                    windows = load_windows(pe, window_regs, batch * G + 2 * G)
                    transposes(batch + 1, after)
                    expand(batch + 1, after, windows)
                    pe.wait_ge(r_lo_ready, batch + 1)
                    pe.wait_ge(acc_steps, batch * G + (G + 2))
                    for v in range(G):
                        nc.tensor.matmul(bank_seg[:, v, :], onehot[:, slot, v, :], r_hi[:, slot, v, :], start=True, stop=False)
                        nc.tensor.matmul(bank_seg[:, v, 0:F], onehot[:, slot, v, :], r_mid[:, slot, v, :], start=False, stop=False)
                        last = nc.tensor.matmul(bank_seg[:, v, 0:F], onehot[:, slot, v, :], r_lo[:, slot, v, :], start=False, stop=True)
                    last.then_inc(sums_in_psum, 1)
            for step in range(GROUPS + 1):
                if step < GROUPS:
                    g, n = step, group_windows(step)
                    pe.wait_ge(sums_packed, g + 1)
                    if g >= 2:
                        pe.wait_ge(sums_t_ready, g - 1)
                    for k in range(n // 2):
                        w = g * GROUP + 2 * k
                        last = nc.tensor.transpose(bank[g % 2][:, k * P:(k + 1) * P], sums[:, w * F:(w + 2) * F], ident)
                    last.then_inc(sums_t_in_psum, 1)
                if step >= 1:
                    g, n = step - 1, group_windows(step - 1)
                    pe.wait_ge(sums_t_ready, g + 1)
                    if g >= 2:
                        pe.wait_ge(out_ready, g - 1)
                    for k in range(n // 2):
                        last = nc.tensor.matmul(bank[2 + g % 2][:, k * P:(k + 1) * P], sums[:, g * GROUP * F + k * P:g * GROUP * F + (k + 1) * P], w2d[:, :], start=True, stop=True)
                    last.then_inc(product_in_psum, 1)

def kernel(x, src, dst, edge_weight1, L0_gnn_W1, L0_gnn_b1, L0_gnn_W2, L0_gnn_b2):
    import numpy as np
    import concourse.bacc as bacc
    from concourse import mybir as mb
    from concourse.bass_utils import run_bass_kernel_spmd

    P = 128
    nodes, feats = x.shape
    edges = src.shape[0]
    cols = lambda a: np.ascontiguousarray(np.asarray(a).reshape(-1, P).T)
    consts = np.concatenate([
        np.eye(P, dtype=np.float32),
        np.tile(np.arange(P, dtype=np.float32), (P, 1)),
        np.triu(np.ones((P, P), np.float32), 1),
        np.arange(1, P + 1, dtype=np.float32)[:, None],
    ], axis=1)
    arrays = {
        "x_in": np.ascontiguousarray(x), "src_cols": cols(src), "dst_cols": cols(dst),
        "edge_cols": cols(edge_weight1), "dst_flat": np.ascontiguousarray(dst),
        "w1": np.ascontiguousarray(L0_gnn_W1), "b1": np.ascontiguousarray(L0_gnn_b1),
        "w2": np.ascontiguousarray(L0_gnn_W2), "b2": np.ascontiguousarray(L0_gnn_b2), "consts": consts,
    }
    nc = bacc.Bacc("TRN2", target_bir_lowering=False, num_devices=1)
    args = [nc.dram_tensor(n, a.shape, mb.dt.from_np(a.dtype), kind="ExternalInput").ap() for n, a in arrays.items()]
    out = nc.dram_tensor("out", (nodes, feats), mb.dt.float32, kind="ExternalOutput").ap()
    preln_gnn_layer(nc, *args, out, nodes, edges)
    r = run_bass_kernel_spmd(nc, [arrays], core_ids=[0])
    return r.results[0]["out"]
```
